# Optimizing a Trainium2 kernel written in Bass

```python
import numpy as np
import jax
import jax.numpy as jnp

def _softmax(x, axis=-1):
    return jax.nn.softmax(x, axis=axis)

def _gelu(x):
    return jax.nn.gelu(x, approximate=True)

def _silu(x):
    return jax.nn.silu(x)

def _sigmoid(x):
    return jax.nn.sigmoid(x)

def _layernorm(x, axis=-1, eps=1e-05):
    m = jnp.mean(x, axis=axis, keepdims=True)
    v = jnp.var(x, axis=axis, keepdims=True)
    return (x - m) / jnp.sqrt(v + eps)

def _scatter_add(tgt, idx, src, axis=0):
    return tgt.at[idx].add(src)

def _segment_sum(src, seg, n):
    return jax.ops.segment_sum(src, seg, n)
kernel_name = 'mk_macaron_d1_jaxref_r8_aeec90'

def setup_inputs(seed: int=0):
    np.random.seed(seed)
    _w = jnp.asarray

    def _L0_attn_setup():
        import jax, jax.numpy as jnp
        import numpy as np
        B, L, D, P = (4, 512, 128, 32)
        EPS = 1e-08

        def _feature_map(x):
            return jax.nn.elu(x) + 1.0
        key = jax.random.key(seed)
        kx, kq, kk, kv, kp = jax.random.split(key, 5)
        x = jax.random.normal(kx, (B, L, D), dtype=jnp.float32)
        scale = 1.0 / np.sqrt(D)
        Wq = jax.random.uniform(kq, (D, D), jnp.float32, -scale, scale)
        Wk = jax.random.uniform(kk, (D, D), jnp.float32, -scale, scale)
        Wv = jax.random.uniform(kv, (D, D), jnp.float32, -scale, scale)
        g = jax.random.normal(kp, (D, P), dtype=jnp.float32)
        proj, _ = jnp.linalg.qr(g, mode='reduced')
        return {'x': x, 'Wq': Wq, 'Wk': Wk, 'Wv': Wv, 'proj': proj}
    _L0_attn_in = _L0_attn_setup()

    def _L0_ffn_setup():
        import jax, jax.numpy as jnp
        import numpy as np
        D_MODEL = 128
        D_FF = 512
        N_EXPERTS = 4
        key = jax.random.key(seed)
        ks = jax.random.split(key, 8)
        s_in = 1.0 / np.sqrt(D_MODEL)
        s_ff = 1.0 / np.sqrt(D_FF)
        x = jax.random.normal(ks[0], (4, 256, D_MODEL), dtype=jnp.float32)
        W1 = jax.random.uniform(ks[1], (N_EXPERTS, D_MODEL, D_FF), jnp.float32, -s_in, s_in)
        b1 = jax.random.uniform(ks[2], (N_EXPERTS, D_FF), jnp.float32, -s_in, s_in)
        W2 = jax.random.uniform(ks[3], (N_EXPERTS, D_FF, D_MODEL), jnp.float32, -s_ff, s_ff)
        b2 = jax.random.uniform(ks[4], (N_EXPERTS, D_MODEL), jnp.float32, -s_ff, s_ff)
        Wg = jax.random.uniform(ks[5], (D_MODEL, N_EXPERTS), jnp.float32, -s_in, s_in)
        bg = jax.random.uniform(ks[6], (N_EXPERTS,), jnp.float32, -s_in, s_in)
        return {'x': x, 'W1': W1, 'b1': b1, 'W2': W2, 'b2': b2, 'Wg': Wg, 'bg': bg}
    _L0_ffn_in = _L0_ffn_setup()
    _d = {'L0_attn_x': _L0_attn_in['x'], 'L0_attn_Wq': _L0_attn_in['Wq'], 'L0_attn_Wk': _L0_attn_in['Wk'], 'L0_attn_Wv': _L0_attn_in['Wv'], 'L0_attn_proj': _L0_attn_in['proj'], 'L0_ffn_W1': _L0_ffn_in['W1'], 'L0_ffn_b1': _L0_ffn_in['b1'], 'L0_ffn_W2': _L0_ffn_in['W2'], 'L0_ffn_b2': _L0_ffn_in['b2'], 'L0_ffn_Wg': _L0_ffn_in['Wg'], 'L0_ffn_bg': _L0_ffn_in['bg']}
    _x0 = _d['L0_attn_x']
    _d['L0_attn_x'] = jax.random.normal(jax.random.fold_in(jax.random.key(seed), 1), (2, 2048, 128), dtype=_x0.dtype)
    del _x0
    return _d

def reference(L0_attn_x, L0_attn_Wq, L0_attn_Wk, L0_attn_Wv, L0_attn_proj, L0_ffn_W1, L0_ffn_b1, L0_ffn_W2, L0_ffn_b2, L0_ffn_Wg, L0_ffn_bg):

    def _L0_attn_ref(x, Wq, Wk, Wv, proj):
        import jax, jax.numpy as jnp
        import numpy as np
        B, L, D, P = (4, 512, 128, 32)
        EPS = 1e-08

        def _feature_map(x):
            return jax.nn.elu(x) + 1.0
        q = jnp.einsum('bld,ed->ble', x, Wq)
        k = jnp.einsum('bld,ed->ble', x, Wk)
        v = jnp.einsum('bld,ed->ble', x, Wv)
        q_prime = _feature_map(q @ proj)
        k_prime = _feature_map(k @ proj)
        kv = jnp.einsum('blp,bld->bpd', k_prime, v)
        num = jnp.einsum('blp,bpd->bld', q_prime, kv)
        z = 1.0 / (jnp.sum(q_prime, axis=-1, keepdims=True) + EPS)
        return num * z

    def _L0_ffn_ref(x, W1, b1, W2, b2, Wg, bg):
        import jax, jax.numpy as jnp
        import numpy as np
        D_MODEL = 128
        D_FF = 512
        N_EXPERTS = 4
        gate_logits = jnp.einsum('bld,de->ble', x, Wg) + bg
        idx = jnp.argmax(jax.nn.softmax(gate_logits, axis=-1), axis=-1)
        h = jnp.einsum('bld,edf->belf', x, W1) + b1[None, :, None, :]
        h = jax.nn.gelu(h, approximate=False)
        y = jnp.einsum('belf,efd->beld', h, W2) + b2[None, :, None, :]
        onehot = jax.nn.one_hot(idx, N_EXPERTS, dtype=x.dtype)
        out = jnp.einsum('beld,ble->bld', y, onehot)
        return out
    x = L0_attn_x
    x = x + 0.5 * _L0_ffn_ref(_layernorm(x, axis=-1), L0_ffn_W1, L0_ffn_b1, L0_ffn_W2, L0_ffn_b2, L0_ffn_Wg, L0_ffn_bg)
    x = x + _L0_attn_ref(_layernorm(x, axis=-1), L0_attn_Wq, L0_attn_Wk, L0_attn_Wv, L0_attn_proj)
    x = x + 0.5 * _L0_ffn_ref(_layernorm(x, axis=-1), L0_ffn_W1, L0_ffn_b1, L0_ffn_W2, L0_ffn_b2, L0_ffn_Wg, L0_ffn_bg)
    return x

_drawn_inputs = setup_inputs


def setup_inputs(seed=0):
    import zlib

    import numpy as np

    out = dict(_drawn_inputs(seed))
    spreads = {}
    factors = {}
    for name, (base, spread) in spreads.items():
        noise = np.random.default_rng([zlib.crc32(name.encode()), seed]).standard_normal(out[name].shape)
        drawn = base * np.exp(spread * noise) if base else spread * noise
        out[name] = jnp.asarray(drawn.astype(out[name].dtype))
    for name, factor in factors.items():
        out[name] = (out[name] * factor).astype(out[name].dtype)
    return out
```

```python
import concourse.bass as bass
from concourse import mybir
from contextlib import ExitStack


class Step:

    def __init__(self, j, k, r, unroll):
        self.j, self.k, self.r, self.unroll = j, k, r, unroll

    def plus(self, d):
        k = self.k + d
        return Step(self.j + d, k % self.unroll, self.r + k // self.unroll, self.unroll)


def run_steps(eng, n, unroll, body, loop_end=None):
    loops = ((n if loop_end is None else loop_end) - unroll) // unroll
    for j in range(unroll):
        body(Step(j, j % unroll, j // unroll, unroll))
    if loops > 0:
        with eng.Fori(1, 1 + loops) as i:
            for u in range(unroll):
                body(Step(i * unroll + u, u, i, unroll))
    for j in range(unroll * (1 + loops), n):
        body(Step(j, j % unroll, j // unroll, unroll))


class Stage:

    def __init__(self, sem, credit=0):
        self.sem, self.credit = sem, credit

    def open(self, eng):
        eng.sem_inc(self.sem, self.credit)

    def done(self, instruction):
        instruction.then_inc(self.sem, 1)


def need(eng, stage, j):
    if isinstance(j, int) and j < 0:
        return
    eng.wait_ge(stage.sem, j + (1 + stage.credit))


def build(nc, x, wq, wk, wv, proj, w1, b1, w2, b2, wg, bg, out):
    f32, bf16, i32 = mybir.dt.float32, mybir.dt.bfloat16, mybir.dt.int32
    ALU, ACT, AX = mybir.AluOpType, mybir.ActivationFunctionType, mybir.AxisListType

    P = 128
    B, L, D = x.shape
    TOKENS = B * L
    NE, _, F = w1.shape
    R = proj.shape[1]
    NC = F // P
    T0 = TOKENS // P
    T1 = T0 + NE - 1
    GS0, GS1 = 4, 5
    NG0, NG1 = T0 // GS0, T1 // GS1
    EPS_LN, EPS_Z = 1e-5, 1e-8
    FAR = 2 * TOKENS
    CREDIT, CREDITED = 4, ("xT", "mm", "lg", "gt", "feat", "qt", "qts", "num")
    assert D == P and T1 % GS1 == 0 and T0 % GS0 == 0 and B == 2

    x_rows = x.rearrange("b l d -> (b l) d").rearrange("(p t) d -> p t d", t=T0)
    out_rows = out.rearrange("b l d -> (b l) d")
    rows0 = nc.dram_tensor("rows0", (TOKENS, 2 * D), f32, kind="Internal").ap()
    rows1 = nc.dram_tensor("rows1", (P * T1, 2 * D), f32, kind="Internal").ap()
    rows0_v = rows0.rearrange("(p t) (c d) -> p t c d", t=T0, c=2)
    rows1_v = rows1.rearrange("(p t) (c d) -> p t c d", t=T1, c=2)

    with ExitStack() as ctx:
        def sb(name, shape, dt=f32):
            return ctx.enter_context(nc.sbuf_tensor(name, shape, dt))

        def sem(name):
            return ctx.enter_context(nc.semaphore(name))

        def stage(name):
            return Stage(sem("s_" + name), CREDIT if name.split("_")[-1] in CREDITED else 0)

        W1 = sb("W1", [P, NE * F])
        W2 = sb("W2", [P, NE * F])
        B1 = sb("B1", [P, NE * F])
        B2 = sb("B2", [P, NE, F])
        Wg = sb("Wg", [P, NE])
        Bg = sb("Bg", [P, NE])
        Wq = sb("Wq", [P, D])
        Wk = sb("Wk", [P, D])
        Wv = sb("Wv", [P, D])
        Pr = sb("Pr", [P, R])
        Wkq = sb("Wkq", [P, 2 * R])
        WvT = sb("WvT", [P, D])
        ident = sb("ident", [P, P])
        below = sb("below", [P, P])
        below_b = sb("below_b", [P, P], bf16)
        ones_b = sb("ones_b", [P, P], bf16)
        zeros = sb("zeros", [P, NE * T1])
        neghalf = sb("neghalf", [P, GS1])
        lane_i = sb("lane_i", [P, P], i32)
        lane_b = sb("lane_b", [P, P], bf16)
        lane_f = sb("lane_f", [P, T1])
        part_i = sb("part_i", [P, 1], i32)
        part1 = sb("part1", [P, 1])
        exp_no_i = sb("exp_no_i", [P, NE, T1], i32)
        exp_no = sb("exp_no", [P, NE, T1])

        X0 = sb("X0", [P, T0, D])
        X1 = sb("X1", [P, T1, D])
        QT = sb("QT", [B * R, T1 * P])
        DEN = sb("DEN", [P, T1])
        Z = sb("Z", [P, T1])
        xn = [sb(f"xn{i}", [P, GS1, D]) for i in range(2)]
        xnT = [sb(f"xnT{i}", [P, GS1, P]) for i in range(2)]
        stats = [sb(f"stats{i}", [P, GS1, 6]) for i in range(2)]
        mv = [sb(f"mv{i}", [P, GS1, 2]) for i in range(2)]
        ve = [sb(f"ve{i}", [P, GS1]) for i in range(2)]
        nmean = [sb(f"nmean{i}", [P, GS1]) for i in range(2)]
        nmr = [sb(f"nmr{i}", [P, GS1]) for i in range(2)]
        rstd = [sb(f"rstd{i}", [P, GS1]) for i in range(2)]
        expo = [sb(f"expo{i}", [P, GS1, 2 * R]) for i in range(2)]
        relu = [sb(f"relu{i}", [P, GS1, 2 * R]) for i in range(2)]
        feat = [sb(f"feat{i}", [P, GS1, 2 * R]) for i in range(2)]
        kmask = [sb(f"kmask{i}", [P, GS1, B, R]) for i in range(2)]
        qmask = [sb(f"qmask{i}", [P, GS1, B, R]) for i in range(2)]
        batch = sb("batch", [P, T1, B])
        qs = [sb(f"qs{i}", [B * R, GS1 * P]) for i in range(2)]
        GT = sb("GT", [P, B * R])
        KV = sb("KV", [B * R, D])

        lg = sb("lg", [P, NE, T1])
        top = sb("top", [P, T1])
        eq = sb("eq", [P, NE, T1])
        pref = sb("pref", [P, NE, T1])
        first = sb("first", [P, T1])
        hot = sb("hot", [P, NE, T1])
        hot_b = sb("hot_b", [P, NE, T1], bf16)
        cum = sb("cum", [P, NE * T1])
        ends = sb("ends", [P, NE + 1])
        cnt_i = sb("cnt_i", [P, NE], i32)
        til_i = sb("til_i", [P, NE], i32)
        til = sb("til", [P, NE])
        tend = sb("tend", [P, NE])
        tstart = sb("tstart", [P, NE])
        base = sb("base", [P, NE])
        where = sb("where", [P, NE, T1])
        where2 = sb("where2", [P, NE, T1])
        where3 = sb("where3", [P, NE, T1])
        pos = sb("pos", [P, T1])
        posx = sb("posx", [P, T1])
        pos_i = sb("pos_i", [P, T1], i32)
        tile_i = sb("tile_i", [P, T1], i32)
        slot_i = sb("slot_i", [P, T1], i32)
        tile_f = sb("tile_f", [P, T1])
        slot_b = sb("slot_b", [P, T1], bf16)
        AV = sb("AV", [P, T1, 5, T1], bf16)
        SL = sb("SL", [P, T1, P], bf16)
        ge = sb("ge", [P, 3, T1])
        gsum = sb("gsum", [P, T1])
        tab = sb("tab", [P, 4, T1])
        tmp_a = sb("tmp_a", [P, T1])
        tmp_b = sb("tmp_b", [P, T1])
        tmp_c = sb("tmp_c", [P, T1])
        tmp_d = sb("tmp_d", [P, T1])
        tmp_e = sb("tmp_e", [P, T1])
        empty = sb("empty", [P, T1])
        expert = [sb(f"expert{i}", [P, T1], i32) for i in range(2)]
        src = [sb(f"src{i}", [P, T1], i32) for i in range(2)]
        dst = sb("dst", [P, T1], i32)
        UV = sb("UV", [P, 2, T1])

        U = 4
        g_in = [sb(f"g_in{i}", [P, 2 * D]) for i in range(U)]
        g_idx = [sb(f"g_idx{i}", [P, 1], i32) for i in range(U)]
        o_idx = [sb(f"o_idx{i}", [P, 1], i32) for i in range(U)]
        res = [sb(f"res{i}", [P, D]) for i in range(U)]
        o_out = [sb(f"o_out{i}", [P, D]) for i in range(U)]
        hT_in = [sb(f"hT_in{i}", [P, P]) for i in range(2)]
        hb = [sb(f"hb{i}", [P, F]) for i in range(2)]
        hg = [sb(f"hg{i}", [P, F]) for i in range(2)]
        hT = [sb(f"hT{i}", [P, F]) for i in range(2)]

        PA, PB, PC, PD = (ctx.enter_context(nc.psum_tensor(n, [P, 1024], f32)) for n in ("PA", "PB", "PC", "PD"))

        def bank(area, i, n):
            return area[:, 512 * i:512 * i + n]

        s_w = {n: sem("s_w_" + n) for n in ("w1", "w2", "b1", "b2", "wg", "bg", "wq", "wk", "wv", "pr")}
        s_x = [sem(f"s_xload{i}") for i in range(4)]
        s_r0 = sem("s_r0")
        s_r0n = [sem(f"s_r0n{i}") for i in range(2)]
        s_r1n = [sem(f"s_r1n{i}") for i in range(2)]
        s_r1x = sem("s_r1x")
        s_gate = {e.engine: sem(f"s_gate{n}") for n, e in enumerate((nc.gpsimd, nc.vector, nc.tensor, nc.scalar, nc.sync))}
        s_c = sem("s_c")
        s_cd = sem("s_cd")
        s_setup_pe = sem("s_setup_pe")
        s_setup_dve = sem("s_setup_dve")

        def stages(prefix, names):
            return {n: stage(f"{prefix}_{n}") for n in names.split()}

        ln0, lnA, lnB = (stages(n, "stat mean ve rstd nm nmr xn xT xTs mm lg") for n in ("ln0", "lnA", "lnB"))
        s_kexp, s_krelu, s_feat, s_km, s_qm, s_den, s_gt, s_qt, s_qts = (
            stage(n) for n in ("kexp", "krelu", "feat", "km", "qm", "den", "gt", "qt", "qts"))
        s_mid = sem("s_mid")
        s_qs = stage("qs")
        s_midd = sem("s_midd")
        s_num, s_x2 = stage("num"), stage("x2")

        class Route:
            def __init__(self, n):
                self.d = sem(f"s_{n}_d")
                self.pe = sem(f"s_{n}_pe")
                self.n = 0

        rt = [Route("rt0"), Route("rt1")]

        ffn = [stages(f"f{i}", "idx oidx xT xTs up hb hg gT gTs down res out") for i in range(2)]
        s_gather = [[sem(f"s_gather{f}_{i}") for i in range(U)] for f in range(2)]
        s_scatter = [sem(f"s_scatter_{i}") for i in range(U)]

        block = ctx.enter_context(nc.Block())

        def alone(eng):
            eng.sem_inc(s_gate[eng.engine])


        def ln_dve(eng, ln, SRC, gs, st, also=None):
            k = st.k
            need(eng, ln["nmr"], st.j - 2)
            alone(eng)
            for t in range(gs):
                i = eng.bn_stats(stats[k][:, t, :], SRC[:, bass.ds(st.j * gs + t, 1), :].rearrange("p a d -> p (a d)"))
            ln["stat"].done(i)
            need(eng, ln["stat"], st.j)
            alone(eng)
            for t in range(gs):
                i = eng.bn_aggr(mv[k][:, t, :], stats[k][:, t, :])
            ln["mean"].done(i)

        def ln_pool(eng, ln, gs, st):
            k = st.k
            need(eng, ln["mean"], st.j)
            alone(eng)
            ln["ve"].done(eng.tensor_scalar(ve[k][:, 0:gs], mv[k][:, 0:gs, 1], EPS_LN, None, ALU.add))
            need(eng, ln["ve"], st.j)
            ln["rstd"].done(eng.tensor_tensor(rstd[k][:, 0:gs], ve[k][:, 0:gs], neghalf[:, 0:gs], ALU.pow))
            ln["nm"].done(eng.tensor_scalar(nmean[k][:, 0:gs], mv[k][:, 0:gs, 0], -1.0, None, ALU.mult))
            need(eng, ln["rstd"], st.j)
            need(eng, ln["nm"], st.j)
            ln["nmr"].done(eng.tensor_tensor(nmr[k][:, 0:gs], nmean[k][:, 0:gs], rstd[k][:, 0:gs], ALU.mult))

        def ln_norm(eng, ln, SRC, gs, st, wait_dma):
            k = st.k
            need(eng, ln["nmr"], st.j)
            need(eng, ln["xT"], st.j - 2)
            wait_dma(eng, st)
            alone(eng)
            for t in range(gs):
                i = eng.activation(xn[k][:, t, :], SRC[:, bass.ds(st.j * gs + t, 1), :].rearrange("p a d -> p (a d)"),
                                   ACT.Identity, bias=nmr[k][:, t:t + 1], scale=rstd[k][:, t:t + 1])
            ln["xn"].done(i)

        def ln_pe_transpose(eng, ln, gs, st):
            need(eng, ln["xn"], st.j)
            need(eng, ln["xTs"], st.j - 1)
            for t in range(gs):
                i = eng.transpose(PA[:, t * P:(t + 1) * P], xn[st.k][:, t, :], ident[:, :])
            ln["xT"].done(i)

        def ln_act(eng, ln, gs, st):
            need(eng, ln["xT"], st.j)
            need(eng, ln["mm"], st.j - 2)
            ln["xTs"].done(eng.activation(xnT[st.k][:, 0:gs, :].rearrange("p t d -> p (t d)"), PA[:, 0:gs * P], ACT.Copy))

        def gate_pe(eng, ln, gs, st):
            need(eng, ln["xTs"], st.j)
            need(eng, ln["lg"], st.j - 2)
            for t in range(gs):
                i = eng.matmul(PB[:, 512 * st.k + t * NE:512 * st.k + (t + 1) * NE], xnT[st.k][:, t, :], Wg[:, :],
                               start=True, stop=True)
            ln["mm"].done(i)

        def gate_dve(eng, ln, gs, st):
            need(eng, ln["mm"], st.j)
            ln["lg"].done(eng.tensor_tensor(lg[:, :, bass.ds(st.j * gs, gs)],
                                         PB[:, 512 * st.k:512 * st.k + gs * NE].rearrange("p (t e) -> p e t", e=NE),
                                         Bg[:, :].unsqueeze(2).to_broadcast([P, NE, gs]), ALU.add))

        def skewed(eng, n, parts):
            most = max(l for l, _ in parts)
            def at(st):
                for lag, body in parts:
                    body(st.plus(-lag))
            for j in range(2):
                for lag, body in parts:
                    if j - lag >= 0:
                        body(Step(j - lag, (j - lag) % 2, (j - lag) // 2, 2))
            loops = (n - 2) // 2
            with eng.Fori(1, 1 + loops) as i:
                for u in range(2):
                    at(Step(i * 2 + u, u, i, 2))
            for j in range(2 * (1 + loops), n + most):
                for lag, body in parts:
                    if j - lag < n and j - lag >= 0:
                        body(Step(j - lag, (j - lag) % 2, (j - lag) // 2, 2))


        def route_dve(eng, f):
            r, T = rt[f], (T0, T1)[f]
            n = [0]
            def did(i):
                i.then_inc(r.d, 1)
                n[0] += 1
                eng.wait_ge(r.d, n[0])
            def te(a):
                return a[:, :, 0:T].rearrange("p e t -> p t e")
            def over_e(a):
                return a[:, 0:T].unsqueeze(1).to_broadcast([P, NE, T])
            need(eng, (ln0, lnB)[f]["lg"], (NG0, NG1)[f] - 1)
            did(eng.tensor_reduce(top[:, 0:T], te(lg), AX.X, ALU.max))
            did(eng.tensor_tensor(eq[:, :, 0:T], lg[:, :, 0:T], over_e(top), ALU.is_ge))
            did(eng.scalar_tensor_tensor(out=pref[:, :, 0:T], in0=eq[:, :, 0:T], scalar=-8.0, in1=exp_no[:, :, 0:T],
                                         op0=ALU.mult, op1=ALU.add))
            did(eng.tensor_reduce(first[:, 0:T], te(pref), AX.X, ALU.min))
            did(eng.tensor_tensor(hot[:, :, 0:T], pref[:, :, 0:T], over_e(first), ALU.is_equal))
            if f:
                did(eng.tensor_scalar(tmp_a[:, :], empty[:, :], -1.0, 1.0, ALU.mult, ALU.add))
                did(eng.tensor_tensor(hot[:, :, :], hot[:, :, :], over_e(tmp_a), ALU.mult))
            hb_v = hot_b[:, :, :].rearrange("p e t -> p (e t)")[:, 0:NE * T]
            did(eng.tensor_copy(hb_v.rearrange("p (e t) -> p e t", e=NE), hot[:, :, 0:T]))
            assert n[0] == HOT_AT[f]
            eng.wait_ge(r.pe, 1)
            did(eng.tensor_tensor_scan(cum[:, 0:NE * T], PC[:, 0:NE * T], zeros[:, 0:NE * T], 0.0, ALU.add, ALU.add))
            did(eng.memset(ends[:, 0:1], 0.0))
            did(eng.tensor_copy(ends[:, 1:NE + 1], cum[:, 0:NE * T].rearrange("p (e t) -> p e t", e=NE)[:, :, T - 1]))
            did(eng.tensor_tensor(til[:, :], ends[:, 1:NE + 1], ends[:, 0:NE], ALU.subtract))
            did(eng.tensor_scalar(cnt_i[:, :], til[:, :], float(P - 1), None, ALU.add))
            did(eng.tensor_scalar(til_i[:, :], cnt_i[:, :], 7, None, ALU.arith_shift_right))
            did(eng.tensor_copy(til[:, :], til_i[:, :]))
            did(eng.tensor_tensor_scan(tend[:, :], til[:, :], zeros[:, 0:NE], 0.0, ALU.add, ALU.add))
            did(eng.tensor_tensor(tstart[:, :], tend[:, :], til[:, :], ALU.subtract))
            did(eng.scalar_tensor_tensor(out=base[:, :], in0=tstart[:, :], scalar=float(P), in1=ends[:, 0:NE],
                                         op0=ALU.mult, op1=ALU.subtract))
            did(eng.tensor_tensor(where[:, :, 0:T], cum[:, 0:NE * T].rearrange("p (e t) -> p e t", e=NE),
                                  base[:, :].unsqueeze(2).to_broadcast([P, NE, T]), ALU.add))
            did(eng.tensor_tensor(where2[:, :, 0:T], where[:, :, 0:T],
                                  PC[:, 512:512 + NE * T].rearrange("p (e t) -> p e t", e=NE), ALU.add))
            did(eng.tensor_tensor(where3[:, :, 0:T], where2[:, :, 0:T], hot[:, :, 0:T], ALU.mult))
            did(eng.tensor_reduce(pos[:, 0:T], te(where3), AX.X, ALU.add))
            p_ = pos
            if f:
                did(eng.scalar_tensor_tensor(out=posx[:, :], in0=empty[:, :], scalar=float(FAR), in1=pos[:, :],
                                             op0=ALU.mult, op1=ALU.add))
                p_ = posx
            did(eng.tensor_copy(pos_i[:, 0:T], p_[:, 0:T]))
            did(eng.tensor_scalar(tile_i[:, 0:T], pos_i[:, 0:T], 7, None, ALU.arith_shift_right))
            did(eng.tensor_scalar(slot_i[:, 0:T], pos_i[:, 0:T], P - 1, None, ALU.bitwise_and))
            did(eng.tensor_copy(tile_f[:, 0:T], tile_i[:, 0:T]))
            did(eng.tensor_copy(slot_b[:, 0:T], slot_i[:, 0:T]))
            a1 = AV[:, 0:T, 0, :]
            did(eng.tensor_tensor(a1, tile_f[:, 0:T].unsqueeze(2).to_broadcast([P, T, T1]),
                                  lane_f[:, :].unsqueeze(1).to_broadcast([P, T, T1]), ALU.is_equal))
            did(eng.tensor_scalar(AV[:, 0:T, 1, :], a1, part1[:, 0:1], None, ALU.mult))
            did(eng.tensor_tensor(AV[:, 0:T, 2, :], a1, lane_f[:, 0:T].unsqueeze(2).to_broadcast([P, T, T1]), ALU.mult))
            if f:
                for c in range(2):
                    did(eng.tensor_tensor(AV[:, :, 3 + c, :], a1, UV[:, c, :].unsqueeze(2).to_broadcast([P, T, T1]),
                                          ALU.mult))
            did(eng.tensor_tensor(SL[:, 0:T, :], slot_b[:, 0:T].unsqueeze(2).to_broadcast([P, T, P]),
                                  lane_b[:, :].unsqueeze(1).to_broadcast([P, T, P]), ALU.is_equal))
            assert n[0] == SL_AT[f]
            for e in range(1, NE):
                did(eng.tensor_scalar(ge[:, e - 1, :], lane_f[:, :], tstart[:, e:e + 1], float(F), ALU.is_ge, ALU.mult))
            did(eng.tensor_tensor(gsum[:, :], ge[:, 0, :], ge[:, 1, :], ALU.add))
            did(eng.tensor_tensor(expert[f][:, :], gsum[:, :], ge[:, 2, :], ALU.add))
            eng.wait_ge(r.pe, 2)
            nt = 4 if f else 2
            did(eng.tensor_copy(tab[:, 0:nt, :], PC[:, 0:nt * T1].rearrange("p (c t) -> p c t", t=T1)))
            did(eng.tensor_scalar(tmp_a[:, :], tab[:, 0, :], -1.0, float(T), ALU.add, ALU.mult))
            did(eng.tensor_tensor(tmp_b[:, :], tmp_a[:, :], tab[:, 1, :], ALU.add))
            did(eng.tensor_scalar(src[f][:, :], tmp_b[:, :], 0.0, None, ALU.max))
            did(eng.tensor_scalar(tmp_c[:, :], tab[:, 0, :], 0.0, None, ALU.is_equal))
            if f == 0:
                did(eng.tensor_copy(empty[:, :], tmp_c[:, :]))
                did(eng.tensor_copy(UV[:, :, :], tab[:, 0:2, :]))
                did(eng.tensor_scalar(batch[:, :, 1], tab[:, 0, :], float(P // 2 + 1), None, ALU.is_ge))
                did(eng.tensor_tensor(tmp_d[:, :], tmp_c[:, :], batch[:, :, 1], ALU.add))
                did(eng.tensor_scalar(batch[:, :, 0], tmp_d[:, :], -1.0, 1.0, ALU.mult, ALU.add))
            else:
                did(eng.tensor_scalar(tmp_d[:, :], tab[:, 2, :], -1.0, float(T0), ALU.add, ALU.mult))
                did(eng.tensor_tensor(tmp_e[:, :], tmp_d[:, :], tab[:, 3, :], ALU.add))
                did(eng.scalar_tensor_tensor(out=dst[:, :], in0=tmp_c[:, :], scalar=float(FAR), in1=tmp_e[:, :],
                                             op0=ALU.mult, op1=ALU.add))
            assert n[0] == DONE_AT[f]

        def route_pe(eng, f):
            r, T = rt[f], (T0, T1)[f]
            hb_v = hot_b[:, :, :].rearrange("p e t -> p (e t)")[:, 0:NE * T]
            eng.wait_ge(r.d, HOT_AT[f])
            eng.matmul(PC[:, 0:NE * T], ones_b[:, :], hb_v, start=True, stop=True)
            eng.matmul(PC[:, 512:512 + NE * T], below_b[:, :], hb_v, start=True, stop=True).then_inc(r.pe, 1)
            eng.wait_ge(r.d, SL_AT[f])
            nt = (4 if f else 2) * T1

            def av(t):
                return AV[:, bass.ds(t, 1), 1:(5 if f else 3), :].rearrange("p a c t -> p (a c t)")

            def sl(t):
                return SL[:, bass.ds(t, 1), :].rearrange("p a s -> p (a s)")
            eng.matmul(PC[:, 0:nt], sl(0), av(0), start=True, stop=False)
            with eng.Fori(1, T - 1) as t:
                eng.matmul(PC[:, 0:nt], sl(t), av(t), start=False, stop=False)
            eng.matmul(PC[:, 0:nt], sl(T - 1), av(T - 1), start=False, stop=True).then_inc(r.pe, 1)

        HOT_AT = [6, 8]
        SL_AT = [29, 34]
        DONE_AT = [44, 47]


        def ffn_pool(eng, f):
            s = ffn[f]
            rows = (rows0, rows1)[f]
            eng.wait_ge(rt[f].d, DONE_AT[f])
            if f == 0:
                eng.wait_ge(s_r0, 16)
                for k in range(2):
                    eng.wait_ge(s_r0n[k], 16 * (NG0 // 2))
            else:
                eng.wait_ge(s_r1x, 16 * NG1)
                for k in range(2):
                    eng.wait_ge(s_r1n[k], 16 * ((NG1 + 1 - k) // 2))

            def gather(st):
                k = st.k
                need(eng, s["xT"], st.j - U)
                need(eng, s["res"], st.j - U)
                alone(eng)
                s["idx"].done(eng.tensor_copy(g_idx[k][:, :], src[f][:, bass.ds(st.j, 1)]))
                need(eng, s["idx"], st.j)
                alone(eng)
                eng.indirect_dma_start(out=g_in[k][:, :], out_offset=None, in_=rows,
                                       in_offset=bass.IndirectOffsetOnAxis(ap=g_idx[k][:, 0:1], axis=0))\
                   .then_inc(s_gather[f][k], 16)

            def scatter(st):
                k = st.k
                if not (isinstance(st.r, int) and st.r < 1):
                    eng.wait_ge(s_scatter[k], 16 * st.r)
                    alone(eng)
                s["oidx"].done(eng.tensor_copy(o_idx[k][:, :], dst[:, bass.ds(st.j, 1)]))
                need(eng, s["oidx"], st.j)
                need(eng, s["out"], st.j)
                alone(eng)
                eng.indirect_dma_start(out=out_rows, out_offset=bass.IndirectOffsetOnAxis(ap=o_idx[k][:, 0:1], axis=0),
                                       in_=o_out[k][:, :], in_offset=None,
                                       bounds_check=TOKENS - 1, oob_is_err=False).then_inc(s_scatter[k], 16)

            if f == 0:
                run_steps(eng, T1, U, gather)
            else:
                for j in range(U):
                    gather(Step(j, j, 0, U))
                for j in range(U):
                    gather(Step(j + U, j, 1, U))
                    scatter(Step(j, j, 0, U))
                loops = T1 // U - 2
                with eng.Fori(1, 1 + loops) as i:
                    for u in range(U):
                        gather(Step(i * U + U + u, u, i + 1, U))
                        scatter(Step(i * U + u, u, i, U))
                for j in range((1 + loops) * U, T1):
                    if j + U < T1:
                        gather(Step(j + U, j % U, j // U + 1, U))
                    scatter(Step(j, j % U, j // U, U))
                for k in range(U):
                    eng.wait_ge(s_scatter[k], 16 * ((T1 - k + U - 1) // U))

        def ffn_pe(eng, f):
            s = ffn[f]
            ex = expert[f]
            if f == 0:
                for n in ("w1", "w2"):
                    eng.wait_ge(s_w[n], 16 if n == "w1" else 16 * NE)
            eng.wait_ge(rt[f].d, DONE_AT[f])

            def e_of(j):
                return eng.value_load(ex[0:1, bass.ds(j, 1)], min_val=0, max_val=(NE - 1) * F)

            def turn_in(st):
                k2 = st.k % 2
                eng.wait_ge(s_gather[f][st.k], 16 * st.r + 16)
                need(eng, s["xTs"], st.j - 2)
                s["xT"].done(eng.transpose(bank(PD, k2, P), g_in[st.k][:, 0:D], ident[:, :]))

            def up(st):
                k2 = st.k % 2
                e = e_of(st.j)
                need(eng, s["xTs"], st.j)
                need(eng, s["hb"], st.j - 2)
                s["up"].done(eng.matmul(bank(PA, k2, F), hT_in[k2][:, :], W1[:, bass.ds(e, F)], start=True, stop=True))

            def turn_h(st):
                k2 = st.k % 2
                need(eng, s["hg"], st.j)
                need(eng, s["gTs"], st.j - 2)
                for c in range(NC):
                    i = eng.transpose(PB[:, 512 * k2 + c * P:512 * k2 + (c + 1) * P], hg[k2][:, c * P:(c + 1) * P], ident[:, :])
                s["gT"].done(i)

            def down(st):
                k2 = st.k % 2
                e = e_of(st.j)
                need(eng, s["gTs"], st.j)
                need(eng, s["out"], st.j - 2)
                for c in range(NC):
                    i = eng.matmul(bank(PC, k2, D), hT[k2][:, c * P:(c + 1) * P], W2[:, bass.ds(e + c * P, D)],
                                   start=(c == 0), stop=(c == NC - 1))
                s["down"].done(i)

            for j in range(3):
                turn_in(Step(j, j, 0, U))
            up(Step(0, 0, 0, U))
            up(Step(1, 1, 0, U))

            def body(st):
                turn_h(st)
                if not isinstance(st.j, int) or st.j + 3 < T1:
                    turn_in(st.plus(3))
                if not isinstance(st.j, int) or st.j + 2 < T1:
                    up(st.plus(2))
                down(st)
            run_steps(eng, T1, U, body, loop_end=T1 - 3)

        def ffn_act(eng, f):
            s = ffn[f]

            def copy_in(st):
                need(eng, s["xT"], st.j)
                need(eng, s["up"], st.j - 2)
                s["xTs"].done(eng.activation(hT_in[st.k % 2][:, :], bank(PD, st.k % 2, P), ACT.Copy))

            def gelu(st):
                need(eng, s["hb"], st.j)
                need(eng, s["gT"], st.j - 2)
                s["hg"].done(eng.activation(hg[st.k % 2][:, :], hb[st.k % 2][:, :], ACT.Gelu))

            def copy_h(st):
                need(eng, s["gT"], st.j)
                need(eng, s["down"], st.j - 2)
                s["gTs"].done(eng.activation(hT[st.k % 2][:, :], bank(PB, st.k % 2, F), ACT.Copy))

            for j in range(3):
                copy_in(Step(j, j, 0, U))
            gelu(Step(0, 0, 0, U))
            gelu(Step(1, 1, 0, U))

            def body(st):
                copy_h(st)
                if not isinstance(st.j, int) or st.j + 3 < T1:
                    copy_in(st.plus(3))
                if not isinstance(st.j, int) or st.j + 2 < T1:
                    gelu(st.plus(2))
            run_steps(eng, T1, U, body, loop_end=T1 - 3)

        def ffn_dve(eng, f):
            s = ffn[f]
            ex = expert[f]

            def e_of(j):
                return eng.value_load(ex[0:1, bass.ds(j, 1)], min_val=0, max_val=(NE - 1) * F)

            def bias(st):
                k2 = st.k % 2
                e = e_of(st.j)
                need(eng, s["up"], st.j)
                need(eng, s["hg"], st.j - 2)
                s["hb"].done(eng.tensor_tensor(hb[k2][:, :], bank(PA, k2, F), B1[:, bass.ds(e, F)], ALU.add))
                eng.wait_ge(s_gather[f][st.k], 16 * st.r + 16)
                need(eng, s["out"], st.j - U)
                s["res"].done(eng.tensor_tensor(res[st.k][:, :], g_in[st.k][:, D:2 * D],
                                             B2[:, :, :].rearrange("p e f -> p (e f)")[:, bass.ds(e, D)], ALU.add))

            def finish(st):
                need(eng, s["down"], st.j)
                need(eng, s["res"], st.j)
                if f == 0:
                    o = X1[:, bass.ds(st.j, 1), :].rearrange("p a d -> p (a d)")
                else:
                    o = o_out[st.k][:, :]
                    if not (isinstance(st.r, int) and st.r < 1):
                        eng.wait_ge(s_scatter[st.k], 16 * st.r)
                s["out"].done(eng.scalar_tensor_tensor(out=o, in0=bank(PC, st.k % 2, D), scalar=0.5, in1=res[st.k][:, :],
                                                    op0=ALU.mult, op1=ALU.add))

            bias(Step(0, 0, 0, U))
            bias(Step(1, 1, 0, U))

            def body(st):
                if not isinstance(st.j, int) or st.j + 2 < T1:
                    bias(st.plus(2))
                finish(st)
            run_steps(eng, T1, U, body, loop_end=T1 - 3)


        @block.sync
        def _(eng):
            q = T0 // 4
            for i in range(4):
                eng.dma_start(X0[:, i * q:(i + 1) * q, :], x_rows[:, i * q:(i + 1) * q, :]).then_inc(s_x[i], 16)
            eng.dma_start(Wg[:, :], wg).then_inc(s_w["wg"], 16)
            eng.dma_start(Bg[:, :], bg.unsqueeze(0).to_broadcast([P, NE])).then_inc(s_w["bg"], 16)
            for n, t, a in (("wq", Wq, wq), ("wk", Wk, wk), ("wv", Wv, wv), ("pr", Pr, proj)):
                eng.dma_start(t[:, :], a).then_inc(s_w[n], 16)
            for i in range(4):
                eng.wait_ge(s_x[i], 16)
            eng.dma_start(rows0_v[:, :, 1, :], X0[:, :, :]).then_inc(s_r0, 16)

            def store0(st):
                need(eng, ln0["xn"], st.j)
                alone(eng)
                eng.dma_start(rows0_v[:, bass.ds(st.j * GS0, GS0), 0, :], xn[st.k][:, 0:GS0, :]).then_inc(s_r0n[st.k], 16)
            run_steps(eng, NG0, 2, store0)

            def store1(st):
                need(eng, s_x2, st.j)
                alone(eng)
                eng.dma_start(rows1_v[:, bass.ds(st.j * GS1, GS1), 1, :], X1[:, bass.ds(st.j * GS1, GS1), :]).then_inc(s_r1x, 16)
                need(eng, lnB["xn"], st.j)
                alone(eng)
                eng.dma_start(rows1_v[:, bass.ds(st.j * GS1, GS1), 0, :], xn[st.k][:, :, :]).then_inc(s_r1n[st.k], 16)
            run_steps(eng, NG1, 2, store1)

        @block.gpsimd
        def _(eng):
            eng.memset(ident[:, :], 0.0).then_inc(s_c, 1)
            eng.memset(below[:, :], -1.0).then_inc(s_c, 1)
            eng.memset(neghalf[:, :], -0.5).then_inc(s_c, 1)
            eng.wait_ge(s_c, 3)
            eng.affine_select(out=ident[:, :], in_=ident[:, :], compare_op=ALU.not_equal, fill=1.0, base=0,
                              pattern=[[-1, P]], channel_multiplier=1).then_inc(s_c, 1)
            eng.affine_select(out=below[:, :], in_=below[:, :], compare_op=ALU.is_ge, fill=0.0, base=0,
                              pattern=[[-1, P]], channel_multiplier=1).then_inc(s_c, 1)
            eng.iota(lane_i[:, :], pattern=[[1, P]], base=0, channel_multiplier=0).then_inc(s_c, 1)
            eng.iota(part_i[:, :], pattern=[[1, 1]], base=1, channel_multiplier=1).then_inc(s_c, 1)
            eng.iota(exp_no_i[:, :, :], pattern=[[1, NE], [0, T1]], base=0, channel_multiplier=0).then_inc(s_c, 1)

            run_steps(eng, NG0, 2, lambda st: ln_pool(eng, ln0, GS0, st))
            ffn_pool(eng, 0)

            run_steps(eng, NG1, 2, lambda st: ln_pool(eng, lnA, GS1, st))
            run_steps(eng, NG1, 2, lambda st: ln_pool(eng, lnB, GS1, st))
            ffn_pool(eng, 1)

        @block.vector
        def _(eng):
            for st in (ln0["lg"], lnB["lg"], s_feat, s_qts):
                st.open(eng)
            eng.wait_ge(s_c, 8)
            eng.memset(ones_b[:, :], 1.0).then_inc(s_cd, 1)
            eng.memset(zeros[:, :], 0.0).then_inc(s_cd, 1)
            eng.tensor_copy(below_b[:, :], below[:, :]).then_inc(s_cd, 1)
            eng.tensor_copy(lane_b[:, :], lane_i[:, :]).then_inc(s_cd, 1)
            eng.tensor_copy(lane_f[:, :], lane_i[:, 0:T1]).then_inc(s_cd, 1)
            eng.tensor_copy(part1[:, :], part_i[:, :]).then_inc(s_cd, 1)
            eng.tensor_copy(exp_no[:, :, :], exp_no_i[:, :, :]).then_inc(s_cd, 1)
            for i in range(4):
                eng.wait_ge(s_x[i], 16)
            eng.wait_ge(s_w["bg"], 16)
            skewed(eng, NG0, [(0, lambda st: ln_dve(eng, ln0, X0, GS0, st)), (1, lambda st: gate_dve(eng, ln0, GS0, st))])
            eng.wait_ge(s_setup_pe, 1)
            eng.tensor_copy(Wkq[:, :], PD[:, 0:2 * R]).then_inc(s_setup_dve, 1)
            eng.tensor_copy(WvT[:, :], PD[:, 512:512 + D]).then_inc(s_setup_dve, 1)
            route_dve(eng, 0)
            eng.wait_ge(s_w["b1"], 16)
            eng.wait_ge(s_w["b2"], 16)
            eng.tensor_scalar(B2[:, :, 0:D], B2[:, :, 0:D], 0.5, None, ALU.mult).then_inc(s_setup_dve, 1)
            eng.wait_ge(s_setup_dve, 3)
            ffn_dve(eng, 0)

            def featA(st):
                k = st.k
                kq = PB[:, 512 * k:512 * k + GS1 * 2 * R].rearrange("p (t c) -> p t c", t=GS1)
                need(eng, lnA["mm"], st.j)
                s_krelu.done(eng.tensor_scalar(relu[k][:, :, :], kq, 0.0, None, ALU.max))
                need(eng, s_krelu, st.j)
                need(eng, s_kexp, st.j)
                s_feat.done(eng.scalar_tensor_tensor(out=feat[k][:, :, :], in0=expo[k][:, :, :], scalar=1.0,
                                                     in1=relu[k][:, :, :], op0=ALU.min, op1=ALU.add))
                need(eng, s_feat, st.j)
                need(eng, s_gt, st.j - 2)
                m = batch[:, bass.ds(st.j * GS1, GS1), :].unsqueeze(3).to_broadcast([P, GS1, B, R])
                s_km.done(eng.tensor_tensor(kmask[k][:, :, :, :],
                                            feat[k][:, :, 0:R].unsqueeze(2).to_broadcast([P, GS1, B, R]), m, ALU.mult))
                need(eng, s_qt, st.j - 2)
                s_qm.done(eng.tensor_tensor(qmask[k][:, :, :, :],
                                            feat[k][:, :, R:2 * R].unsqueeze(2).to_broadcast([P, GS1, B, R]), m, ALU.mult))
                s_den.done(eng.tensor_reduce(DEN[:, bass.ds(st.j * GS1, GS1)], feat[k][:, :, R:2 * R], AX.X, ALU.add))

            def qtA(st):
                need(eng, s_qt, st.j)
                s_qts.done(eng.tensor_copy(QT[:, bass.ds(st.j * (GS1 * P), GS1 * P)], PD[0:B * R, 0:GS1 * P]))

            skewed(eng, NG1, [(0, lambda st: ln_dve(eng, lnA, X1, GS1, st)), (1, featA), (2, qtA)])
            need(eng, s_gt, NG1 - 1)
            eng.tensor_copy(GT[:, :], PC[:, 0:B * R]).then_inc(s_midd, 1)
            eng.tensor_scalar(DEN[:, :], DEN[:, :], EPS_Z, None, ALU.add).then_inc(s_midd, 1)
            eng.wait_ge(s_midd, 2)
            eng.reciprocal(Z[:, :], DEN[:, :]).then_inc(s_midd, 1)
            eng.wait_ge(s_mid, 1)
            eng.tensor_copy(KV[:, :], PC[0:B * R, 512:512 + D]).then_inc(s_midd, 1)
            eng.wait_ge(s_midd, 4)

            def x2(st):
                need(eng, s_num, st.j)
                for t in range(GS1):
                    xt = X1[:, bass.ds(st.j * GS1 + t, 1), :].rearrange("p a d -> p (a d)")
                    i = eng.scalar_tensor_tensor(out=xt, in0=PC[:, t * P:(t + 1) * P],
                                                 scalar=Z[:, bass.ds(st.j * GS1 + t, 1)], in1=xt, op0=ALU.mult, op1=ALU.add)
                s_x2.done(i)
                need(eng, s_x2, st.j)
                ln_dve(eng, lnB, X1, GS1, st)
            skewed(eng, NG1, [(0, x2), (1, lambda st: gate_dve(eng, lnB, GS1, st))])
            route_dve(eng, 1)
            ffn_dve(eng, 1)

        @block.tensor
        def _(eng):
            for st in (ln0["xT"], ln0["mm"], lnA["xT"], lnA["mm"], lnB["xT"], lnB["mm"], ffn[0]["xT"], ffn[1]["xT"],
                       s_gt, s_qt, s_num):
                st.open(eng)
            eng.wait_ge(s_c, 8)
            eng.wait_ge(s_cd, 7)
            eng.wait_ge(s_w["wg"], 16)
            run_steps(eng, NG0, 2, lambda st: (ln_pe_transpose(eng, ln0, GS0, st), gate_pe(eng, ln0, GS0, st)))
            for n in ("wq", "wk", "wv", "pr"):
                eng.wait_ge(s_w[n], 16)
            eng.matmul(PD[:, 0:R], Wk[:, :], Pr[:, :], start=True, stop=True)
            eng.matmul(PD[:, R:2 * R], Wq[:, :], Pr[:, :], start=True, stop=True)
            eng.transpose(PD[:, 512:512 + D], Wv[:, :], ident[:, :]).then_inc(s_setup_pe, 1)
            route_pe(eng, 0)
            eng.wait_ge(s_setup_dve, 2)
            ffn_pe(eng, 0)

            def trA(st):
                ln_pe_transpose(eng, lnA, GS1, st)
                need(eng, lnA["xTs"], st.j)
                need(eng, s_krelu, st.j - 2)
                need(eng, s_kexp, st.j - 2)
                for t in range(GS1):
                    i = eng.matmul(PB[:, 512 * st.k + t * 2 * R:512 * st.k + (t + 1) * 2 * R], xnT[st.k][:, t, :], Wkq[:, :],
                                   start=True, stop=True)
                lnA["mm"].done(i)

            def accA(st):
                need(eng, s_km, st.j)
                for t in range(GS1):
                    first = isinstance(st.j, int) and st.j == 0 and t == 0
                    last = isinstance(st.j, int) and st.j == NG1 - 1 and t == GS1 - 1
                    i = eng.matmul(PC[:, 0:B * R], xn[st.k][:, t, :],
                                   kmask[st.k][:, t, :, :].rearrange("p b r -> p (b r)"), start=first, stop=last)
                s_gt.done(i)
                need(eng, s_qm, st.j)
                need(eng, s_qts, st.j - 1)
                alone(eng)
                for t in range(GS1):
                    i = eng.transpose(PD[0:B * R, t * P:(t + 1) * P],
                                      qmask[st.k][:, t, :, :].rearrange("p b r -> p (b r)"), ident[:, :])
                s_qt.done(i)
            skewed(eng, NG1, [(0, trA), (1, accA)])
            eng.wait_ge(s_midd, 1)
            eng.matmul(PC[0:B * R, 512:512 + D], GT[:, :], WvT[:, :], start=True, stop=True).then_inc(s_mid, 1)
            eng.wait_ge(s_midd, 4)

            def num(st):
                need(eng, s_qs, st.j)
                need(eng, s_x2, st.j - 1)
                for t in range(GS1):
                    i = eng.matmul(PC[:, t * P:(t + 1) * P], qs[st.k][:, t * P:(t + 1) * P], KV[:, :], start=True, stop=True)
                s_num.done(i)
            skewed(eng, NG1, [(0, num), (1, lambda st: (ln_pe_transpose(eng, lnB, GS1, st), gate_pe(eng, lnB, GS1, st)))])
            route_pe(eng, 1)
            ffn_pe(eng, 1)

        @block.scalar
        def _(eng):
            w1_v, w2_v = W1[:, :].rearrange("p (e f) -> p e f", e=NE), W2[:, :].rearrange("p (e c d) -> p e c d", e=NE, c=NC)
            eng.dma_start(w1_v, w1.rearrange("e d f -> d e f")).then_inc(s_w["w1"], 16)
            for e in range(NE):
                eng.dma_start(w2_v[:, e, :, :], w2[e, :, :].rearrange("(c p) d -> p c d", p=P)).then_inc(s_w["w2"], 16)
            eng.dma_start(B1[:, :], b1.rearrange("e f -> (e f)").unsqueeze(0).to_broadcast([P, NE * F])).then_inc(s_w["b1"], 16)
            eng.dma_start(B2[:, :, 0:D], b2.unsqueeze(0).to_broadcast([P, NE, D])).then_inc(s_w["b2"], 16)
            for i in range(4):
                eng.wait_ge(s_x[i], 16)

            def stored(sems):
                def wait(e, st):
                    if not (isinstance(st.r, int) and st.r < 1):
                        e.wait_ge(sems[st.k], 16 * st.r)
                return wait
            skewed(eng, NG0, [(1, lambda st: ln_act(eng, ln0, GS0, st)),
                              (0, lambda st: ln_norm(eng, ln0, X0, GS0, st, stored(s_r0n)))])
            ffn_act(eng, 0)

            def expA(st):
                need(eng, s_krelu, st.j)
                need(eng, s_feat, st.j - 2)
                s_kexp.done(eng.activation(expo[st.k][:, :, :].rearrange("p t c -> p (t c)"),
                                           PB[:, 512 * st.k:512 * st.k + GS1 * 2 * R], ACT.Exp))
            for k in range(2):
                eng.wait_ge(s_r0n[k], 16 * (NG0 // 2))
            skewed(eng, NG1, [(1, lambda st: ln_act(eng, lnA, GS1, st)), (2, expA),
                              (0, lambda st: ln_norm(eng, lnA, X1, GS1, st, lambda e, st: need(e, s_gt, st.j - 2)))])
            need(eng, s_qts, NG1 - 1)

            def stage_q(st):
                need(eng, s_num, st.j - 2)
                s_qs.done(eng.activation(qs[st.k][:, :], QT[:, bass.ds(st.j * (GS1 * P), GS1 * P)], ACT.Copy))
            stage_q(Step(0, 0, 0, 2))

            def q_ahead(st):
                if not isinstance(st.j, int) or st.j + 1 < NG1:
                    stage_q(st.plus(1))
            skewed(eng, NG1, [(0, q_ahead), (1, lambda st: ln_act(eng, lnB, GS1, st)),
                              (0, lambda st: ln_norm(eng, lnB, X1, GS1, st, stored(s_r1n)))])
            ffn_act(eng, 1)


_INS = ['L0_attn_x', 'L0_attn_Wq', 'L0_attn_Wk', 'L0_attn_Wv', 'L0_attn_proj',
        'L0_ffn_W1', 'L0_ffn_b1', 'L0_ffn_W2', 'L0_ffn_b2', 'L0_ffn_Wg', 'L0_ffn_bg']


def kernel(**inputs):
    import numpy as _np
    import concourse.bacc as _bacc
    from concourse import mybir as _mybir
    from concourse.bass_utils import run_bass_kernel_spmd as _run

    nc = _bacc.Bacc("TRN2", target_bir_lowering=False, num_devices=1)
    arrays, args = {}, []
    for name in _INS:
        a = _np.ascontiguousarray(inputs[name])
        arrays[f"in_{name}_dram"] = a
        args.append(nc.dram_tensor(f"in_{name}_dram", a.shape, _mybir.dt.from_np(a.dtype), kind="ExternalInput").ap())
    shape = arrays["in_L0_attn_x_dram"].shape
    args.append(nc.dram_tensor("out_0_dram", shape, _mybir.dt.float32, kind="ExternalOutput").ap())
    build(nc, *args)
    r = _run(nc, [arrays], core_ids=[0])
    return r.results[0]["out_0_dram"]
```

```python
import concourse.bass as bass
from concourse import mybir
from contextlib import ExitStack


class Step:

    def __init__(self, j, k, turns16, bufs):
        self.j, self.k, self.turns16, self.bufs = j, k, turns16, bufs

    def plus(self, d):
        k = self.k + d
        return Step(self.j + d, k % self.bufs, self.turns16 + 16 * (k // self.bufs), self.bufs)

    def at_most(self, last):
        return not isinstance(self.j, int) or self.j <= last


def step_of(j, bufs):
    return Step(j, j % bufs, 16 * (j // bufs), bufs)


def run_steps(eng, head, loop_end, n, bufs, body, enter=None, before_loop=None):
    assert head % bufs == 0 and (loop_end - head) % bufs == 0
    shared = None
    for j in range(head):
        if enter and j % bufs == 0:
            shared = enter(j)
        body(step_of(j, bufs), shared)
    if before_loop:
        before_loop()
    with eng.Fori(head, loop_end - bufs + 1, bufs) as i:
        shared = enter(i) if enter else None
        for u in range(bufs):
            body(Step(i + u, u, i * (16 // bufs), bufs), shared)
    for j in range(loop_end, n):
        if enter and j % bufs == 0:
            shared = enter(j)
        body(step_of(j, bufs), shared)


def run_groups(eng, n, parts, before=None):
    most = max(lag for lag, _ in parts)
    loops = (n - 3) // 2

    def peeled(s):
        if before:
            before(s)
        for lag, body in parts:
            if 0 <= s - lag < n:
                body(step_of(s - lag, 2))
    for s in range(3):
        peeled(s)
    if before:
        before(3)
    with eng.Fori(3, 2 + 2 * loops, 2) as i:
        for u in range(2):
            st = Step(i + u, (1 + u) % 2, (i - 1) * 8 + 16 * ((1 + u) // 2), 2)
            for lag, body in parts:
                body(st.plus(-lag))
    for s in range(3 + 2 * loops, n + most):
        for lag, body in parts:
            if 0 <= s - lag < n:
                body(step_of(s - lag, 2))


class Stage:

    def __init__(self, sem):
        self.sem = sem

    def done(self, instruction):
        instruction.then_inc(self.sem, 1)


def need(eng, stage, j):
    if isinstance(j, int) and j < 0:
        return
    eng.wait_ge(stage.sem, j + 1)


def build(nc, x, wq, wk, wv, proj, w1, b1, w2, b2, wg, bg, out):
    f32, bf16, i32 = mybir.dt.float32, mybir.dt.bfloat16, mybir.dt.int32
    ALU, ACT, AX = mybir.AluOpType, mybir.ActivationFunctionType, mybir.AxisListType

    P = 128
    B, L, D = x.shape
    TOKENS = B * L
    NE, _, F = w1.shape
    R = proj.shape[1]
    NC = F // P
    T0 = TOKENS // P
    T1 = T0 + NE - 1
    GS0, GS1 = 4, 5
    NG0, NG1 = T0 // GS0, T1 // GS1
    U = 4
    EPS_LN, EPS_Z = 1e-5, 1e-8
    FAR = 2 * TOKENS
    BANK = 512
    assert D == P and T1 % GS1 == 0 and T0 % GS0 == 0 and B == 2 and B * R <= P

    x_rows = x.rearrange("b l d -> (b l) d").rearrange("(p t) d -> p t d", t=T0)
    out_rows = out.rearrange("b l d -> (b l) d")
    RW0, RW1 = 2 * D, 2 * D + 1
    rows0 = nc.dram_tensor("rows0", (TOKENS, RW0), f32, kind="Internal").ap()
    rows1 = nc.dram_tensor("rows1", (P * T1 + 1, RW1), f32, kind="Internal").ap()
    rows0_v = rows0.rearrange("(p t) c -> p t c", t=T0)
    rows1_v = rows1[0:P * T1, :].rearrange("(p t) c -> p t c", t=T1)

    with ExitStack() as ctx:
        def sb(name, shape, dt=f32):
            return ctx.enter_context(nc.sbuf_tensor(name, shape, dt))

        def pair(name, shape, dt=f32, n=2):
            return [sb(f"{name}{i}", shape, dt) for i in range(n)]

        def sem(name):
            return ctx.enter_context(nc.semaphore(name))

        def stages(prefix, names):
            return {n: Stage(sem(f"s_{prefix}_{n}")) for n in names.split()}

        W1 = sb("W1", [P, NE * F])
        W2 = sb("W2", [P, NE * F])
        B1 = sb("B1", [P, NE * F])
        B2 = sb("B2", [P, NE * F])
        Wg = sb("Wg", [P, NE])
        Bg = sb("Bg", [P, NE])
        Wq = sb("Wq", [P, D])
        Wk = sb("Wk", [P, D])
        Wv = sb("Wv", [P, D])
        Pr = sb("Pr", [P, R])
        Wkq = sb("Wkq", [P, 2 * R])
        WvT = sb("WvT", [P, D])
        ident = sb("ident", [P, P])
        below = sb("below", [P, P])
        below_b = sb("below_b", [P, P], bf16)
        ones_b = sb("ones_b", [P, P], bf16)
        zeros = sb("zeros", [P, NE * T1])
        neghalf = sb("neghalf", [P, T1])
        lane_i = sb("lane_i", [P, P], i32)
        lane_b = sb("lane_b", [P, P], bf16)
        lane_f = sb("lane_f", [P, T1])
        part_i = sb("part_i", [P, 1], i32)
        part1 = sb("part1", [P, 1])
        exp_no_i = sb("exp_no_i", [P, NE, T1], i32)
        exp_no = sb("exp_no", [P, NE, T1])
        padrow = sb("padrow", [1, RW1])
        warm = sb("warm", [P, 1])

        X0 = sb("X0", [P, T0, D])
        X1 = sb("X1", [P, T1, D + 1])
        STATS = sb("STATS", [P, T1, 6])
        MR = sb("MR", [P, T1, 2])
        QT = sb("QT", [B * R, T1 * P])
        DEN = sb("DEN", [P, T1])
        DENE = sb("DENE", [P, T1])
        Z = sb("Z", [P, T1])
        batch = sb("batch", [P, T1, B])
        xn = pair("xn", [P, GS1, D])
        xnT = pair("xnT", [P, GS1 * P])
        stats = pair("stats", [P, GS1, 6])
        mv = pair("mv", [P, GS1, 2])
        mr = pair("mr", [P, GS1, 2])
        ve = pair("ve", [P, GS1])
        rstd = pair("rstd", [P, GS1])
        nmean = pair("nmean", [P, GS1])
        nmr = pair("nmr", [P, GS1])
        expo = pair("expo", [P, GS1, 2 * R])
        relu = pair("relu", [P, GS1, 2 * R])
        feat = pair("feat", [P, GS1, 2 * R])
        kmask = pair("kmask", [P, GS1, B * R])
        qmask = pair("qmask", [P, GS1, B * R])
        qs = pair("qs", [B * R, GS1 * P])
        GT = sb("GT", [P, B * R])
        KV = sb("KV", [B * R, D])

        lg = sb("lg", [P, NE, T1])
        hot_b = sb("hot_b", [P, NE * T1], bf16)
        cum = sb("cum", [P, NE * T1])
        AV = sb("AV", [P, T1, 3, T1], bf16)
        SL = sb("SL", [P, T1, P], bf16)
        cnt_i, til_i = sb("cnt_i", [P, NE], i32), sb("til_i", [P, NE], i32)
        ends = sb("ends", [P, NE + 1])
        cnt, til, tend, tstart, base = (sb(n, [P, NE]) for n in ("cnt", "til", "tend", "tstart", "base"))
        eq, pref, hot, hot2, where, where2, where3 = (
            sb(n, [P, NE, T1]) for n in ("eq", "pref", "hot", "hot2", "where", "where2", "where3"))
        top, first, filled, pos, posx, tile_f, gsum, ra, rb, rc, rd, empty = (
            sb(n, [P, T1]) for n in ("top", "first", "filled", "pos", "posx", "tile_f", "gsum", "ra", "rb", "rc", "rd",
                                     "empty"))
        pos_i, tile_i, slot_i = (sb(n, [P, T1], i32) for n in ("pos_i", "tile_i", "slot_i"))
        slot_b = sb("slot_b", [P, T1], bf16)
        ge = sb("ge", [P, NE - 1, T1])
        tab = sb("tab", [P, 2, T1])
        expert = pair("expert", [P, T1], i32)
        src = pair("src", [P, T1 + U], i32)


        g_in = pair("g_in", [P, RW1], n=U)
        g_idx = pair("g_idx", [P, 1], i32, n=U)
        token = pair("token", [P, 1], i32, n=U)
        o_idx = pair("o_idx", [P, 1], i32, n=U)
        res = pair("res", [P, D], n=U)
        o_out = pair("o_out", [P, D], n=U)
        hT_in = pair("hT_in", [P, P])
        hb = pair("hb", [P, F])
        hg = pair("hg", [P, F])
        hT = pair("hT", [P, F])

        PA, PB, PC, PD = (ctx.enter_context(nc.psum_tensor(n, [P, 2 * BANK], f32)) for n in ("PA", "PB", "PC", "PD"))

        def bank(area, i, n):
            return area[:, BANK * i:BANK * i + n]

        s_w = {n: sem("s_w_" + n) for n in ("w1", "w2", "b1", "b2", "wg", "bg", "wq", "wk", "wv", "pr")}
        XCH = (0, 2 * GS0, 3 * GS0, T0)
        s_xload = [sem(f"s_xload{i}") for i in range(3)]
        s_rows0x = sem("s_rows0x")
        s_rows0n = [sem(f"s_rows0n{i}") for i in range(2)]
        s_rows1x = [sem(f"s_rows1x{i}") for i in range(2)]
        s_rows1n = [sem(f"s_rows1n{i}") for i in range(2)]
        s_padrow = sem("s_padrow")
        s_const = sem("s_const")
        s_constd = sem("s_constd")
        s_fold = sem("s_fold")
        s_foldd = sem("s_foldd")
        s_warm = sem("s_warm")
        s_mid = sem("s_mid")
        s_midd = sem("s_midd")
        s_alone = {e.engine: sem(f"s_alone{n}")
                   for n, e in enumerate((nc.gpsimd, nc.vector, nc.tensor, nc.scalar, nc.sync))}
        s_rd = [sem(f"s_route_dve{f}") for f in range(2)]
        s_rp = [sem(f"s_route_pe{f}") for f in range(2)]
        l0 = stages("l0", "stat mean ve rstd mr xn xT xTs mm lg")
        la = stages("la", "mr xn xT xTs mm kx feat km den gt qt qts")
        lb = stages("lb", "qs num x2 stat mean ve rstd nm nmr xn xT xTs mm lg")
        ffn = [stages(f"f{i}", "idx xT xTs up hb hg gT gTs down out st") for i in range(2)]
        s_gather = [[sem(f"s_gather{f}_{i}") for i in range(U)] for f in range(2)]
        s_scatter = [sem(f"s_scatter_{i}") for i in range(U)]

        block = ctx.enter_context(nc.Block())

        def alone(eng):
            eng.sem_inc(s_alone[eng.engine])

        def row(a, t, n=D):
            return a[:, bass.ds(t, 1), 0:n].rearrange("p a d -> p (a d)")


        def l0_stats(eng, st):
            k = st.k
            for t in range(GS0):
                i = eng.bn_stats(stats[k][:, t, :], row(X0, st.j * GS0 + t))
            l0["stat"].done(i)
            need(eng, l0["stat"], st.j)
            alone(eng)
            for t in range(GS0):
                i = eng.bn_aggr(mv[k][:, t, :], stats[k][:, t, :])
            l0["mean"].done(i)

        def l0_rstd(eng, st):
            k = st.k
            need(eng, l0["mean"], st.j)
            alone(eng)
            l0["ve"].done(eng.tensor_scalar(ve[k][:, 0:GS0], mv[k][:, 0:GS0, 1], EPS_LN, None, ALU.add))
            need(eng, l0["ve"], st.j)
            l0["rstd"].done(eng.tensor_tensor(rstd[k][:, 0:GS0], ve[k][:, 0:GS0], neghalf[:, 0:GS0], ALU.pow))

        def l0_norm(eng, st):
            k = st.k
            need(eng, l0["rstd"], st.j)
            if not (isinstance(st.j, int) and st.j < 2):
                eng.wait_ge(s_rows0n[k], st.turns16)
            alone(eng)
            for t in range(GS0):
                i = eng.tensor_scalar(xn[k][:, t, :], row(X0, st.j * GS0 + t), mv[k][:, t, 0:1], rstd[k][:, t:t + 1],
                                      ALU.subtract, ALU.mult)
            l0["xn"].done(i)

        def l0_turn(eng, st):
            need(eng, l0["xn"], st.j)
            for t in range(GS0):
                i = eng.transpose(PA[:, BANK * st.k + t * P:BANK * st.k + (t + 1) * P], xn[st.k][:, t, :], ident[:, :])
            l0["xT"].done(i)

        def l0_copy(eng, st):
            need(eng, l0["xT"], st.j)
            l0["xTs"].done(eng.activation(xnT[st.k][:, 0:GS0 * P], bank(PA, st.k, GS0 * P), ACT.Copy))

        def gate_mm(eng, s, gs, st):
            need(eng, s["xTs"], st.j)
            if isinstance(st.j, int):
                need(eng, s["lg"], st.j - 2)
            for t in range(gs):
                i = eng.matmul(PB[:, BANK * st.k + t * NE:BANK * st.k + (t + 1) * NE], xnT[st.k][:, t * P:(t + 1) * P],
                               Wg[:, :], start=True, stop=True)
            s["mm"].done(i)

        def gate_add(eng, s, gs, st):
            need(eng, s["mm"], st.j)
            s["lg"].done(eng.tensor_tensor(lg[:, :, bass.ds(st.j * gs, gs)],
                                           bank(PB, st.k, gs * NE).rearrange("p (t e) -> p e t", e=NE),
                                           Bg[:, :].unsqueeze(2).to_broadcast([P, NE, gs]), ALU.add))

        SPLIT = 7
        AT = [{}, {}]

        def te(a, T):
            return a[:, :, 0:T].rearrange("p e t -> p t e")

        def route_dve(eng, f):
            T, n, at = (T0, T1)[f], [0], AT[f]

            def did(i, chain=True):
                i.then_inc(s_rd[f], 1)
                n[0] += 1
                if chain:
                    eng.wait_ge(s_rd[f], n[0])

            def reached(name):
                assert at[name] == n[0], (name, n[0])

            def over_e(a):
                return a[:, 0:T].unsqueeze(1).to_broadcast([P, NE, T])

            def wide(a):
                return a.unsqueeze(2).to_broadcast([P, T, T1])
            need(eng, (l0, lb)[f]["lg"], (NG0, NG1)[f] - 1)
            did(eng.tensor_reduce(top[:, 0:T], te(lg, T), AX.X, ALU.max))
            did(eng.tensor_tensor(eq[:, :, 0:T], lg[:, :, 0:T], over_e(top), ALU.is_ge))
            did(eng.scalar_tensor_tensor(out=pref[:, :, 0:T], in0=eq[:, :, 0:T], scalar=-8.0, in1=exp_no[:, :, 0:T],
                                         op0=ALU.mult, op1=ALU.add))
            did(eng.tensor_reduce(first[:, 0:T], te(pref, T), AX.X, ALU.min))
            did(eng.tensor_tensor(hot[:, :, 0:T], pref[:, :, 0:T], over_e(first), ALU.is_equal))
            h = hot
            if f:
                did(eng.tensor_tensor(hot2[:, :, :], hot[:, :, :], over_e(filled), ALU.mult))
                h = hot2
            did(eng.tensor_copy(hot_b[:, 0:NE * T].rearrange("p (e t) -> p e t", e=NE), h[:, :, 0:T]))
            reached("hot")
            did(eng.memset(ends[:, 0:1], 0.0), False)
            eng.wait_ge(s_rp[f], 1)
            did(eng.tensor_tensor_scan(cum[:, 0:NE * T], PC[:, 0:NE * T], zeros[:, 0:NE * T], 0.0, ALU.add, ALU.add))
            c3 = cum[:, 0:NE * T].rearrange("p (e t) -> p e t", e=NE)
            did(eng.tensor_copy(ends[:, 1:NE + 1], c3[:, :, T - 1]))
            did(eng.tensor_tensor(cnt[:, :], ends[:, 1:NE + 1], ends[:, 0:NE], ALU.subtract))
            did(eng.tensor_scalar(cnt_i[:, :], cnt[:, :], float(P - 1), None, ALU.add))
            did(eng.tensor_scalar(til_i[:, :], cnt_i[:, :], 7, None, ALU.arith_shift_right))
            did(eng.tensor_copy(til[:, :], til_i[:, :]))
            did(eng.tensor_tensor_scan(tend[:, :], til[:, :], zeros[:, 0:NE], 0.0, ALU.add, ALU.add))
            did(eng.tensor_tensor(tstart[:, :], tend[:, :], til[:, :], ALU.subtract))
            did(eng.scalar_tensor_tensor(out=base[:, :], in0=tstart[:, :], scalar=float(P), in1=ends[:, 0:NE],
                                         op0=ALU.mult, op1=ALU.subtract))
            did(eng.tensor_tensor(where[:, :, 0:T], c3, base[:, :].unsqueeze(2).to_broadcast([P, NE, T]), ALU.add))
            did(eng.tensor_tensor(where2[:, :, 0:T], where[:, :, 0:T],
                                  bank(PC, 1, NE * T).rearrange("p (e t) -> p e t", e=NE), ALU.add))
            did(eng.tensor_tensor(where3[:, :, 0:T], where2[:, :, 0:T], h[:, :, 0:T], ALU.mult))
            did(eng.tensor_reduce(pos[:, 0:T], te(where3, T), AX.X, ALU.add))
            p_ = pos
            if f:
                did(eng.scalar_tensor_tensor(out=posx[:, :], in0=empty[:, :], scalar=float(FAR), in1=pos[:, :],
                                             op0=ALU.mult, op1=ALU.add))
                p_ = posx
            did(eng.tensor_copy(pos_i[:, 0:T], p_[:, 0:T]))
            did(eng.tensor_scalar(tile_i[:, 0:T], pos_i[:, 0:T], 7, None, ALU.arith_shift_right), False)
            did(eng.tensor_scalar(slot_i[:, 0:T], pos_i[:, 0:T], P - 1, None, ALU.bitwise_and))
            did(eng.tensor_copy(tile_f[:, 0:T], tile_i[:, 0:T]), False)
            did(eng.tensor_copy(slot_b[:, 0:T], slot_i[:, 0:T]))
            a1 = AV[:, 0:T, 0, :]
            did(eng.tensor_tensor(a1, wide(tile_f[:, 0:T]), lane_f[:, :].unsqueeze(1).to_broadcast([P, T, T1]),
                                  ALU.is_equal))
            did(eng.tensor_scalar(AV[:, 0:T, 1, :], a1, part1[:, 0:1], None, ALU.mult), False)
            did(eng.tensor_tensor(AV[:, 0:T, 2, :], a1, wide(lane_f[:, 0:T]), ALU.mult), False)
            for c in range(0, T, SPLIT):
                w = min(SPLIT, T - c)
                did(eng.tensor_tensor(SL[:, c:c + w, :], slot_b[:, c:c + w].unsqueeze(2).to_broadcast([P, w, P]),
                                      lane_b[:, :].unsqueeze(1).to_broadcast([P, w, P]), ALU.is_equal), False)
                reached(f"slots{c // SPLIT}")
            for e in range(1, NE):
                did(eng.tensor_scalar(ge[:, e - 1, :], lane_f[:, :], tstart[:, e:e + 1], float(F), ALU.is_ge, ALU.mult),
                    e == NE - 1)
            did(eng.tensor_tensor(gsum[:, :], ge[:, 0, :], ge[:, 1, :], ALU.add))
            did(eng.tensor_tensor(expert[f][:, :], gsum[:, :], ge[:, 2, :], ALU.add), False)
            eng.wait_ge(s_rp[f], 2)
            did(eng.tensor_copy(tab[:, :, :], PC[:, 0:2 * T1].rearrange("p (c t) -> p c t", t=T1)))
            did(eng.tensor_scalar(ra[:, :], tab[:, 0, :], -1.0, float(T), ALU.add, ALU.mult), False)
            did(eng.tensor_scalar(empty[:, :] if f == 0 else rd[:, :], tab[:, 0, :], 0.0, None, ALU.is_equal))
            if f == 0:
                did(eng.tensor_tensor(rb[:, :], ra[:, :], tab[:, 1, :], ALU.add))
                did(eng.tensor_scalar(src[0][:, 0:T1], rb[:, :], 0.0, None, ALU.max), False)
                reached("done")
                did(eng.scalar_tensor_tensor(out=rc[:, :], in0=empty[:, :], scalar=float(FAR), in1=rb[:, :],
                                             op0=ALU.mult, op1=ALU.add), False)
                did(eng.tensor_scalar(filled[:, :], empty[:, :], -1.0, 1.0, ALU.mult, ALU.add), False)
                did(eng.tensor_scalar(batch[:, :, 1], tab[:, 0, :], float(P // B + 1), None, ALU.is_ge))
                did(eng.tensor_copy(X1[:, :, D:D + 1].bitcast(i32).rearrange("p t a -> p (t a)"), rc[:, :]), False)
                did(eng.tensor_tensor(batch[:, :, 0], filled[:, :], batch[:, :, 1], ALU.subtract))
            else:
                did(eng.tensor_tensor(rb[:, :], ra[:, :], tab[:, 1, :], ALU.add), False)
                did(eng.tensor_scalar(rc[:, :], rd[:, :], float((P + 1) * T1), None, ALU.mult))
                did(eng.tensor_tensor(src[1][:, 0:T1], rb[:, :], rc[:, :], ALU.add))
                reached("done")

        def route_counts():
            for f, T in enumerate((T0, T1)):
                c = AT[f]
                c["hot"] = 6 + f
                slots = c["hot"] + 1 + 13 + f + 5 + 3
                for i in range(-(-T // SPLIT)):
                    c[f"slots{i}"] = slots + i + 1
                c["done"] = slots + -(-T // SPLIT) + (NE - 1) + 2 + 3 + (2 if f == 0 else 3)
        route_counts()

        def route_pe(eng, f):
            T = (T0, T1)[f]
            eng.wait_ge(s_rd[f], AT[f]["hot"])
            eng.matmul(PC[:, 0:NE * T], ones_b[:, :], hot_b[:, 0:NE * T], start=True, stop=True)
            eng.matmul(PC[:, BANK:BANK + NE * T], below_b[:, :], hot_b[:, 0:NE * T], start=True, stop=True)\
               .then_inc(s_rp[f], 1)
            for t in range(T):
                if t % SPLIT == 0:
                    eng.wait_ge(s_rd[f], AT[f][f"slots{t // SPLIT}"])
                i = eng.matmul(PC[:, 0:2 * T1], SL[:, t, :], AV[:, t, 1:3, :].rearrange("p c t -> p (c t)"),
                               start=(t == 0), stop=(t == T - 1))
            i.then_inc(s_rp[f], 1)


        def ffn_pool(eng, f):
            s, rows, RW = ffn[f], (rows0, rows1)[f], (RW0, RW1)[f]
            eng.wait_ge(s_rd[f], AT[f]["done"])
            if f == 0:
                eng.wait_ge(s_rows0x, 16)
                for k in range(2):
                    eng.wait_ge(s_rows0n[k], 16 * (NG0 // 2))
            else:
                eng.wait_ge(s_padrow, 16)
                for k in range(2):
                    eng.wait_ge(s_rows1x[k], 16 * ((NG1 + 1 - k) // 2))
                    eng.wait_ge(s_rows1n[k], 16 * ((NG1 + 1 - k) // 2))

            def gather(st):
                k = st.k
                need(eng, s["hb"], st.j - U)
                alone(eng)
                eng.indirect_dma_start(out=g_in[k][:, 0:RW], out_offset=None, in_=rows,
                                       in_offset=bass.IndirectOffsetOnAxis(ap=g_idx[k][:, 0:1], axis=0))\
                   .then_inc(s_gather[f][k], 16)

            def scatter(st):
                k = st.k
                need(eng, s["out"], st.j)
                alone(eng)
                eng.indirect_dma_start(out=out_rows, out_offset=bass.IndirectOffsetOnAxis(ap=o_idx[k][:, 0:1], axis=0),
                                       in_=o_out[k][:, :], in_offset=None,
                                       bounds_check=TOKENS - 1, oob_is_err=False).then_inc(s_scatter[k], 16)

            eng.wait_ge(s["idx"].sem, U)
            if f == 0:
                run_steps(eng, U, T1 - T1 % U, T1, U, lambda st, _: gather(st))
                return
            for j in range(U):
                gather(step_of(j, U))

            def both(st, _):
                if st.at_most(T1 - 1 - U):
                    gather(st.plus(U))
                scatter(st)
            last = T1 - T1 % U - U
            run_steps(eng, U, last, T1, U, both)
            for k in range(U):
                eng.wait_ge(s_scatter[k], 16 * ((T1 - k + U - 1) // U))

        def experts_of(eng, f, j, n):
            _, values = nc.values_load_multi_w_load_instructions(
                expert[f][0:1, bass.ds(j, n)], engines=[eng.engine], min_val=0, max_val=(NE - 1) * F,
                skip_runtime_bounds_check_because="DVE sums at most NE-1 comparisons times F")
            return values

        def ffn_pe(eng, f):
            s = ffn[f]
            ln_at = (RW0, RW1)[f] - D
            if f == 0:
                eng.wait_ge(s_w["w1"], 16)
                eng.wait_ge(s_w["w2"], 16 * NE)
            eng.wait_ge(s_rd[f], AT[f]["done"])

            def turn_in(st):
                eng.wait_ge(s_gather[f][st.k], st.turns16 + 16)
                s["xT"].done(eng.transpose(bank(PD, st.k % 2, P), g_in[st.k][:, ln_at:ln_at + D], ident[:, :]))

            def up(st, e):
                need(eng, s["xTs"], st.j)
                s["up"].done(eng.matmul(bank(PA, st.k % 2, F), hT_in[st.k % 2][:, :], W1[:, bass.ds(e, F)],
                                        start=True, stop=True))

            def turn_h(st):
                k2 = st.k % 2
                need(eng, s["hg"], st.j)
                for c in range(NC):
                    i = eng.transpose(PB[:, BANK * k2 + c * P:BANK * k2 + (c + 1) * P], hg[k2][:, c * P:(c + 1) * P],
                                      ident[:, :])
                s["gT"].done(i)

            def down(st, e):
                k2 = st.k % 2
                need(eng, s["gTs"], st.j)
                for c in range(NC):
                    i = eng.matmul(bank(PC, k2, D), hT[k2][:, c * P:(c + 1) * P], W2[:, bass.ds(e + c * P, D)],
                                   start=(c == 0), stop=(c == NC - 1))
                s["down"].done(i)

            def load(j):
                n = U + 2 if not isinstance(j, int) else min(U + 2, T1 - j)
                return experts_of(eng, f, j, n)
            e0 = load(0)
            for j in range(3):
                turn_in(step_of(j, U))
                if j > 0:
                    up(step_of(j - 1, U), e0[j - 1])

            def body(st, e):
                turn_h(st)
                if st.at_most(T1 - 4):
                    turn_in(st.plus(3))
                if st.at_most(T1 - 3):
                    up(st.plus(2), e[st.k + 2])
                down(st, e[st.k])
            run_steps(eng, U, T1 - 3, T1, U, body, load)

        def ffn_act(eng, f):
            s = ffn[f]

            def copy_in(st):
                need(eng, s["xT"], st.j)
                s["xTs"].done(eng.activation(hT_in[st.k % 2][:, :], bank(PD, st.k % 2, P), ACT.Copy))

            def gelu(st):
                need(eng, s["hb"], st.j)
                s["hg"].done(eng.activation(hg[st.k % 2][:, :], hb[st.k % 2][:, :], ACT.Gelu))

            def copy_h(st):
                need(eng, s["gT"], st.j)
                s["gTs"].done(eng.activation(hT[st.k % 2][:, :], bank(PB, st.k % 2, F), ACT.Copy))
            copy_in(step_of(0, U))
            copy_in(step_of(1, U))
            gelu(step_of(0, U))
            need(eng, s["up"], 0)
            copy_in(step_of(2, U))
            gelu(step_of(1, U))

            def body(st, _):
                copy_h(st)
                if st.at_most(T1 - 4):
                    copy_in(st.plus(3))
                if st.at_most(T1 - 3):
                    gelu(st.plus(2))
            run_steps(eng, U, T1 - 3, T1, U, body)

        def ffn_dve(eng, f):
            s = ffn[f]

            def bias(st, e):
                if f:
                    eng.tensor_copy(token[st.k][:, :], g_in[st.k][:, D:D + 1].bitcast(i32))
                eng.tensor_copy(g_idx[st.k][:, :], src[f][:, bass.ds(st.j + U, 1)])
                eng.tensor_tensor(res[st.k][:, :], g_in[st.k][:, 0:D], B2[:, bass.ds(e, D)], ALU.add)
                s["hb"].done(eng.tensor_tensor(hb[st.k % 2][:, :], bank(PA, st.k % 2, F), B1[:, bass.ds(e, F)], ALU.add))

            def finish(st):
                need(eng, s["down"], st.j)
                if f and not (isinstance(st.j, int) and st.j < U):
                    eng.wait_ge(s_scatter[st.k], st.turns16)
                if f:
                    eng.tensor_copy(o_idx[st.k][:, :], token[st.k][:, :])
                s["out"].done(eng.scalar_tensor_tensor(out=row(X1, st.j) if f == 0 else o_out[st.k][:, :],
                                                       in0=bank(PC, st.k % 2, D), scalar=0.5, in1=res[st.k][:, :],
                                                       op0=ALU.mult, op1=ALU.add))

            def stat(j):
                need(eng, s["out"], j)
                alone(eng)
                s["st"].done(eng.bn_stats(row(STATS, j, 6), row(X1, j)))

            def load(j):
                n = U if not isinstance(j, int) else min(U, T1 - 2 - j)
                return experts_of(eng, f, j + 2, n) if n > 0 else None
            for j in range(U):
                eng.tensor_copy(g_idx[j][:, :], src[f][:, j:j + 1]).then_inc(s["idx"].sem, 1)
            e0 = experts_of(eng, f, 0, 2)
            for j in range(2):
                need(eng, s["up"], j)
                bias(step_of(j, U), e0[j])

            def body(st, e):
                finish(st)
                if st.at_most(T1 - 3):
                    bias(st.plus(2), e[st.k])
                if f == 0 and not (isinstance(st.j, int) and st.j < 1):
                    stat(st.j - 1)
            run_steps(eng, U, T1 - 3, T1, U, body, load)
            if f == 0:
                stat(T1 - 1)


        def la_stats(eng):
            n = [0]

            def did(i):
                i.then_inc(s_midd, 1)
                n[0] += 1
                eng.wait_ge(s_midd, n[0])
            need(eng, ffn[0]["st"], T1 - 1)
            eng.tensor_tensor(ra[:, :], STATS[:, :, 1], STATS[:, :, 4], ALU.add).then_inc(s_midd, 1)
            eng.tensor_tensor(rb[:, :], STATS[:, :, 1], STATS[:, :, 4], ALU.subtract).then_inc(s_midd, 1)
            n[0] = 2
            did(eng.tensor_tensor(rc[:, :], STATS[:, :, 2], STATS[:, :, 5], ALU.add))
            eng.tensor_scalar(MR[:, :, 0], ra[:, :], 0.5, None, ALU.mult).then_inc(s_midd, 1)
            eng.tensor_tensor(rd[:, :], rb[:, :], rb[:, :], ALU.mult).then_inc(s_midd, 1)
            n[0] = 5
            did(eng.tensor_scalar(gsum[:, :], rc[:, :], 1.0 / D, EPS_LN, ALU.mult, ALU.add))
            did(eng.scalar_tensor_tensor(out=ra[:, :], in0=rd[:, :], scalar=0.25, in1=gsum[:, :],
                                         op0=ALU.mult, op1=ALU.add))
        MID_VAR, MID_GT, MID_KV = 7, 8, 11

        def la_norm(eng, st):
            k = st.k
            la["mr"].done(eng.tensor_copy(mr[k][:, :, :], MR[:, bass.ds(st.j * GS1, GS1), :]))
            need(eng, la["gt"], st.j - 2)
            need(eng, la["mr"], st.j)
            alone(eng)
            for t in range(GS1):
                i = eng.tensor_scalar(xn[k][:, t, :], row(X1, st.j * GS1 + t), mr[k][:, t, 0:1], mr[k][:, t, 1:2],
                                      ALU.subtract, ALU.mult)
            la["xn"].done(i)

        def la_features(eng, st):
            k = st.k
            need(eng, la["kx"], st.j)
            la["feat"].done(eng.scalar_tensor_tensor(out=feat[k][:, :, :], in0=expo[k][:, :, :], scalar=1.0,
                                                     in1=relu[k][:, :, :], op0=ALU.min, op1=ALU.add))
            need(eng, la["feat"], st.j)
            m = batch[:, bass.ds(st.j * GS1, GS1), :].unsqueeze(3).to_broadcast([P, GS1, B, R])

            def masked(o, c):
                return eng.tensor_tensor(o[k][:, :, :].rearrange("p t (b r) -> p t b r", b=B),
                                         feat[k][:, :, c:c + R].unsqueeze(2).to_broadcast([P, GS1, B, R]), m, ALU.mult)
            masked(qmask, R)
            la["km"].done(masked(kmask, 0))
            la["den"].done(eng.tensor_reduce(DEN[:, bass.ds(st.j * GS1, GS1)], feat[k][:, :, R:2 * R], AX.X, ALU.add))

        def la_sum(eng, st):
            k = st.k
            need(eng, la["km"], st.j)
            for t in range(GS1):
                i = eng.matmul(PC[:, 0:B * R], xn[k][:, t, :], kmask[k][:, t, :],
                               start=isinstance(st.j, int) and st.j == 0 and t == 0,
                               stop=isinstance(st.j, int) and st.j == NG1 - 1 and t == GS1 - 1)
            la["gt"].done(i)
            for t in range(GS1):
                i = eng.transpose(PD[0:B * R, t * P:(t + 1) * P], qmask[k][:, t, :], ident[:, :])
            la["qt"].done(i)

        def la_mm(eng, st):
            need(eng, la["xTs"], st.j)
            for t in range(GS1):
                i = eng.matmul(PB[:, BANK * st.k + t * 2 * R:BANK * st.k + (t + 1) * 2 * R],
                               xnT[st.k][:, t * P:(t + 1) * P], Wkq[:, :], start=True, stop=True)
            la["mm"].done(i)

        def la_turn(eng, st):
            need(eng, la["xn"], st.j)
            for t in range(GS1):
                i = eng.transpose(PA[:, t * P:(t + 1) * P], xn[st.k][:, t, :], ident[:, :])
            la["xT"].done(i)

        def la_act_q(eng, st):
            need(eng, la["qt"], st.j)
            alone(eng)
            la["qts"].done(eng.activation(QT[:, bass.ds(st.j * (GS1 * P), GS1 * P)], PD[0:B * R, 0:GS1 * P], ACT.Copy))

        def la_act_exp(eng, st):
            k = st.k
            need(eng, la["mm"], st.j)
            v = bank(PB, k, GS1 * 2 * R)
            eng.activation(relu[k][:, :, :].rearrange("p t c -> p (t c)"), v, ACT.Relu)
            la["kx"].done(eng.activation(expo[k][:, :, :].rearrange("p t c -> p (t c)"), v, ACT.Exp))

        def la_act_copy(eng, st):
            need(eng, la["xT"], st.j)
            la["xTs"].done(eng.activation(xnT[st.k][:, :], PA[:, 0:GS1 * P], ACT.Copy))


        def lb_queries(eng, st):
            need(eng, lb["num"], st.j - 2)
            alone(eng)
            lb["qs"].done(eng.tensor_copy(qs[st.k][:, :], QT[:, bass.ds(st.j * (GS1 * P), GS1 * P)]))

        def lb_rstd(eng, st):
            k = st.k
            need(eng, lb["mean"], st.j)
            alone(eng)
            lb["ve"].done(eng.tensor_scalar(ve[k][:, :], mv[k][:, :, 1], EPS_LN, None, ALU.add))
            lb["nm"].done(eng.tensor_scalar(nmean[k][:, :], mv[k][:, :, 0], -1.0, None, ALU.mult))
            need(eng, lb["ve"], st.j)
            lb["rstd"].done(eng.tensor_tensor(rstd[k][:, :], ve[k][:, :], neghalf[:, 0:GS1], ALU.pow))
            need(eng, lb["nm"], st.j)
            need(eng, lb["rstd"], st.j)
            lb["nmr"].done(eng.tensor_tensor(nmr[k][:, :], nmean[k][:, :], rstd[k][:, :], ALU.mult))

        def lb_num(eng, st):
            need(eng, lb["qs"], st.j)
            need(eng, lb["x2"], st.j - 1)
            for t in range(GS1):
                i = eng.matmul(PC[:, t * P:(t + 1) * P], qs[st.k][:, t * P:(t + 1) * P], KV[:, :], start=True, stop=True)
            lb["num"].done(i)

        def lb_turn(eng, st):
            need(eng, lb["xn"], st.j)
            for t in range(GS1):
                i = eng.transpose((PA, PD)[st.k][:, t * P:(t + 1) * P], xn[st.k][:, t, :], ident[:, :])
            lb["xT"].done(i)

        def lb_x2(eng, st):
            k = st.k
            need(eng, lb["num"], st.j)
            for t in range(GS1):
                xt = row(X1, st.j * GS1 + t)
                i = eng.scalar_tensor_tensor(out=xt, in0=PC[:, t * P:(t + 1) * P], scalar=Z[:, bass.ds(st.j * GS1 + t, 1)],
                                             in1=xt, op0=ALU.mult, op1=ALU.add)
            lb["x2"].done(i)
            need(eng, lb["x2"], st.j)
            alone(eng)
            for t in range(GS1):
                i = eng.bn_stats(stats[k][:, t, :], row(X1, st.j * GS1 + t))
            lb["stat"].done(i)
            need(eng, lb["stat"], st.j)
            alone(eng)
            for t in range(GS1):
                i = eng.bn_aggr(mv[k][:, t, :], stats[k][:, t, :])
            lb["mean"].done(i)

        def lb_norm(eng, st):
            k = st.k
            need(eng, lb["nmr"], st.j)
            if not (isinstance(st.j, int) and st.j < 2):
                eng.wait_ge(s_rows1n[k], st.turns16)
            alone(eng)
            for t in range(GS1):
                i = eng.activation(xn[k][:, t, :], row(X1, st.j * GS1 + t), ACT.Identity,
                                   bias=nmr[k][:, t:t + 1], scale=rstd[k][:, t:t + 1])
            lb["xn"].done(i)

        def lb_copy(eng, st):
            need(eng, lb["xT"], st.j)
            lb["xTs"].done(eng.activation(xnT[st.k][:, :], (PA, PD)[st.k][:, 0:GS1 * P], ACT.Copy))


        @block.sync
        def _(eng):
            for i in range(3):
                eng.dma_start(X0[:, XCH[i]:XCH[i + 1], :], x_rows[:, XCH[i]:XCH[i + 1], :]).then_inc(s_xload[i], 16)
            eng.dma_start(Wg[:, :], wg).then_inc(s_w["wg"], 16)
            eng.dma_start(Bg[:, :], bg.unsqueeze(0).to_broadcast([P, NE])).then_inc(s_w["bg"], 16)
            for n, t, a in (("wq", Wq, wq), ("wk", Wk, wk), ("wv", Wv, wv), ("pr", Pr, proj)):
                eng.dma_start(t[:, :], a).then_inc(s_w[n], 16)
            for i in range(3):
                eng.wait_ge(s_xload[i], 16)
            eng.dma_start(rows0_v[:, :, 0:D], X0[:, :, :]).then_inc(s_rows0x, 16)

            def store0(st):
                need(eng, l0["xn"], st.j)
                alone(eng)
                eng.dma_start(rows0_v[:, bass.ds(st.j * GS0, GS0), D:2 * D], xn[st.k][:, 0:GS0, :])\
                   .then_inc(s_rows0n[st.k], 16)
            run_groups(eng, NG0, [(0, store0)])
            eng.wait_ge(s_const, 9)
            eng.dma_start(rows1[P * T1:P * T1 + 1, :], padrow[:, :]).then_inc(s_padrow, 16)

            def store1x(st):
                need(eng, lb["x2"], st.j)
                alone(eng)
                eng.dma_start(rows1_v[:, bass.ds(st.j * GS1, GS1), 0:D + 1], X1[:, bass.ds(st.j * GS1, GS1), :])\
                   .then_inc(s_rows1x[st.k], 16)

            def store1n(st):
                need(eng, lb["xn"], st.j)
                alone(eng)
                eng.dma_start(rows1_v[:, bass.ds(st.j * GS1, GS1), D + 1:RW1], xn[st.k][:, :, :])\
                   .then_inc(s_rows1n[st.k], 16)
            run_groups(eng, NG1, [(0, store1x), (1, store1n)])

        @block.gpsimd
        def _(eng):
            eng.memset(ident[:, :], 0.0).then_inc(s_const, 1)
            eng.memset(below[:, :], -1.0).then_inc(s_const, 1)
            eng.memset(neghalf[:, :], -0.5).then_inc(s_const, 1)
            eng.memset(padrow[:, :], 0.0).then_inc(s_const, 1)
            eng.wait_ge(s_const, 4)
            eng.affine_select(out=ident[:, :], in_=ident[:, :], compare_op=ALU.not_equal, fill=1.0, base=0,
                              pattern=[[-1, P]], channel_multiplier=1).then_inc(s_const, 1)
            eng.affine_select(out=below[:, :], in_=below[:, :], compare_op=ALU.is_ge, fill=0.0, base=0,
                              pattern=[[-1, P]], channel_multiplier=1).then_inc(s_const, 1)
            eng.iota(lane_i[:, :], pattern=[[1, P]], base=0, channel_multiplier=0).then_inc(s_const, 1)
            eng.iota(part_i[:, :], pattern=[[1, 1]], base=1, channel_multiplier=1).then_inc(s_const, 1)
            eng.iota(padrow[:, D:D + 1].bitcast(i32), pattern=[[0, 1]], base=FAR, channel_multiplier=0)\
               .then_inc(s_const, 1)
            eng.iota(exp_no_i[:, :, :], pattern=[[1, NE], [0, T1]], base=0, channel_multiplier=0).then_inc(s_const, 1)
            run_groups(eng, NG0, [(0, lambda st: l0_rstd(eng, st))])
            ffn_pool(eng, 0)
            eng.wait_ge(s_midd, MID_VAR)
            eng.tensor_tensor(MR[:, :, 1], ra[:, :], neghalf[:, :], ALU.pow).then_inc(s_mid, 1)
            need(eng, la["qts"], NG1 - 1)
            run_groups(eng, NG1, [(0, lambda st: lb_queries(eng, st)), (1, lambda st: lb_rstd(eng, st))])
            ffn_pool(eng, 1)

        @block.vector
        def _(eng):
            eng.wait_ge(s_const, 10)
            eng.memset(ones_b[:, :], 1.0).then_inc(s_constd, 1)
            eng.memset(zeros[:, :], 0.0).then_inc(s_constd, 1)
            for f in range(2):
                eng.memset(src[f][:, T1:T1 + U], 0).then_inc(s_constd, 1)
            eng.tensor_copy(below_b[:, :], below[:, :]).then_inc(s_constd, 1)
            eng.tensor_copy(lane_b[:, :], lane_i[:, :]).then_inc(s_constd, 1)
            eng.tensor_copy(lane_f[:, :], lane_i[:, 0:T1]).then_inc(s_constd, 1)
            eng.tensor_copy(part1[:, :], part_i[:, :]).then_inc(s_constd, 1)
            eng.tensor_copy(exp_no[:, :, :], exp_no_i[:, :, :]).then_inc(s_constd, 1)
            eng.wait_ge(s_w["bg"], 16)

            def loaded(s):
                for i in {0: (0,), 2: (1,), 3: (2,)}.get(s, ()):
                    eng.wait_ge(s_xload[i], 16)
            run_groups(eng, NG0, [(0, lambda st: l0_stats(eng, st)), (3, lambda st: gate_add(eng, l0, GS0, st)),
                                  (1, lambda st: l0_norm(eng, st))], loaded)
            route_dve(eng, 0)
            eng.wait_ge(s_w["b1"], 16)
            eng.wait_ge(s_w["b2"], 16)
            b2v = B2[:, :].rearrange("p (e f) -> p e f", e=NE)[:, :, 0:D]
            eng.tensor_scalar(b2v, b2v, 0.5, None, ALU.mult).then_inc(s_foldd, 1)
            eng.wait_ge(s_fold, 1)
            eng.tensor_copy(Wkq[:, :], PD[:, 0:2 * R]).then_inc(s_foldd, 1)
            eng.tensor_copy(WvT[:, :], PD[:, BANK:BANK + D]).then_inc(s_foldd, 1)
            eng.wait_ge(s_foldd, 3)
            ffn_dve(eng, 0)
            la_stats(eng)
            eng.wait_ge(s_mid, 1)
            run_groups(eng, NG1, [(0, lambda st: la_norm(eng, st)), (1, lambda st: la_features(eng, st))])
            need(eng, la["gt"], NG1 - 1)
            eng.tensor_copy(GT[:, :], PC[:, 0:B * R]).then_inc(s_midd, 1)
            need(eng, la["den"], NG1 - 1)
            eng.tensor_scalar(DENE[:, :], DEN[:, :], EPS_Z, None, ALU.add).then_inc(s_midd, 1)
            eng.wait_ge(s_midd, MID_GT + 1)
            eng.reciprocal(Z[:, :], DENE[:, :]).then_inc(s_midd, 1)
            eng.wait_ge(s_mid, 2)
            eng.tensor_copy(KV[:, :], PC[0:B * R, BANK:BANK + D]).then_inc(s_midd, 1)
            eng.wait_ge(s_midd, MID_KV)
            run_groups(eng, NG1, [(0, lambda st: lb_x2(eng, st)), (2, lambda st: gate_add(eng, lb, GS1, st))])
            route_dve(eng, 1)
            ffn_dve(eng, 1)

        @block.tensor
        def _(eng):
            eng.wait_ge(s_const, 10)
            eng.wait_ge(s_constd, 9)
            eng.wait_ge(s_w["wg"], 16)
            run_groups(eng, NG0, [(2, lambda st: gate_mm(eng, l0, GS0, st)), (1, lambda st: l0_turn(eng, st))])
            for n in ("wq", "wk", "wv", "pr"):
                eng.wait_ge(s_w[n], 16)
            eng.matmul(PD[:, 0:R], Wk[:, :], Pr[:, :], start=True, stop=True)
            eng.matmul(PD[:, R:2 * R], Wq[:, :], Pr[:, :], start=True, stop=True)
            eng.transpose(PD[:, BANK:BANK + D], Wv[:, :], ident[:, :]).then_inc(s_fold, 1)
            route_pe(eng, 0)
            eng.wait_ge(s_foldd, 3)
            ffn_pe(eng, 0)
            run_groups(eng, NG1, [(2, lambda st: la_sum(eng, st)), (1, lambda st: la_mm(eng, st)),
                                  (0, lambda st: la_turn(eng, st))])
            eng.wait_ge(s_midd, MID_GT)
            eng.matmul(PC[0:B * R, BANK:BANK + D], GT[:, :], WvT[:, :], start=True, stop=True).then_inc(s_mid, 1)
            eng.wait_ge(s_midd, MID_KV)
            run_groups(eng, NG1, [(0, lambda st: lb_num(eng, st)), (2, lambda st: gate_mm(eng, lb, GS1, st)),
                                  (1, lambda st: lb_turn(eng, st))])
            route_pe(eng, 1)
            ffn_pe(eng, 1)

        @block.scalar
        def _(eng):
            w1_v, w2_v = W1[:, :].rearrange("p (e f) -> p e f", e=NE), W2[:, :].rearrange("p (e c d) -> p e c d", e=NE, c=NC)
            eng.dma_start(w1_v, w1.rearrange("e d f -> d e f")).then_inc(s_w["w1"], 16)
            for e in range(NE):
                eng.dma_start(w2_v[:, e, :, :], w2[e, :, :].rearrange("(c p) d -> p c d", p=P)).then_inc(s_w["w2"], 16)
            eng.dma_start(B1[:, :], b1.rearrange("e f -> (e f)").unsqueeze(0).to_broadcast([P, NE * F])).then_inc(s_w["b1"], 16)
            eng.dma_start(B2[:, :].rearrange("p (e f) -> p e f", e=NE)[:, :, 0:D], b2.unsqueeze(0).to_broadcast([P, NE, D]))\
               .then_inc(s_w["b2"], 16)

            def warm_up(function):
                eng.activation(warm[:, :], neghalf[:, 0:1], function).then_inc(s_warm, 1)
            eng.wait_ge(s_const, 4)
            run_groups(eng, NG0, [(1, lambda st: l0_copy(eng, st))])
            warm_up(ACT.Gelu)
            ffn_act(eng, 0)
            warm_up(ACT.Exp)
            run_groups(eng, NG1, [(2, lambda st: la_act_q(eng, st)), (1, lambda st: la_act_exp(eng, st)),
                                  (0, lambda st: la_act_copy(eng, st))])
            run_groups(eng, NG1, [(2, lambda st: lb_copy(eng, st)), (1, lambda st: lb_norm(eng, st))])
            warm_up(ACT.Gelu)
            ffn_act(eng, 1)


_INS = ['L0_attn_x', 'L0_attn_Wq', 'L0_attn_Wk', 'L0_attn_Wv', 'L0_attn_proj',
        'L0_ffn_W1', 'L0_ffn_b1', 'L0_ffn_W2', 'L0_ffn_b2', 'L0_ffn_Wg', 'L0_ffn_bg']


def kernel(**inputs):
    import numpy as _np
    import concourse.bacc as _bacc
    from concourse import mybir as _mybir
    from concourse.bass_utils import run_bass_kernel_spmd as _run

    nc = _bacc.Bacc("TRN2", target_bir_lowering=False, num_devices=1)
    arrays, args = {}, []
    for name in _INS:
        a = _np.ascontiguousarray(inputs[name])
        arrays[f"in_{name}_dram"] = a
        args.append(nc.dram_tensor(f"in_{name}_dram", a.shape, _mybir.dt.from_np(a.dtype), kind="ExternalInput").ap())
    shape = arrays["in_L0_attn_x_dram"].shape
    args.append(nc.dram_tensor("out_0_dram", shape, _mybir.dt.float32, kind="ExternalOutput").ap())
    build(nc, *args)
    r = _run(nc, [arrays], core_ids=[0])
    return r.results[0]["out_0_dram"]
```

```python
import concourse.bass as bass
from concourse import mybir
from contextlib import ExitStack


class Step:

    def __init__(self, j, k, turns16, bufs):
        self.j, self.k, self.turns16, self.bufs = j, k, turns16, bufs

    def plus(self, d):
        k = self.k + d
        return Step(self.j + d, k % self.bufs, self.turns16 + 16 * (k // self.bufs), self.bufs)

    def at_most(self, last):
        return not isinstance(self.j, int) or self.j <= last


def step_of(j, bufs):
    return Step(j, j % bufs, 16 * (j // bufs), bufs)


def run_steps(eng, head, loop_end, n, bufs, body, enter=None, after_loop=None):
    assert head % bufs == 0 and (loop_end - head) % bufs == 0
    shared = None
    for j in range(head):
        if enter and j % bufs == 0:
            shared = enter(j)
        body(step_of(j, bufs), shared)
    with eng.Fori(head, loop_end - bufs + 1, bufs) as i:
        shared = enter(i) if enter else None
        for u in range(bufs):
            body(Step(i + u, u, i * (16 // bufs), bufs), shared)
    if after_loop:
        after_loop()
    for j in range(loop_end, n):
        if enter and j % bufs == 0:
            shared = enter(j)
        body(step_of(j, bufs), shared)


def run_groups(eng, n, parts, before=None):
    most = max(lag for lag, _ in parts)
    loops = (n - 3) // 2

    def peeled(s):
        if before:
            before(s)
        for lag, body in parts:
            if 0 <= s - lag < n:
                body(step_of(s - lag, 2))
    for s in range(3):
        peeled(s)
    if before:
        before(3)
    with eng.Fori(3, 2 + 2 * loops, 2) as i:
        for u in range(2):
            st = Step(i + u, (1 + u) % 2, (i - 1) * 8 + 16 * ((1 + u) // 2), 2)
            for lag, body in parts:
                body(st.plus(-lag))
    for s in range(3 + 2 * loops, n + most):
        for lag, body in parts:
            if 0 <= s - lag < n:
                body(step_of(s - lag, 2))


class Stage:
    AHEAD = 2

    def __init__(self, sem):
        self.sem = sem

    def done(self, instruction):
        instruction.then_inc(self.sem, 1)


def need(eng, stage, j):
    if isinstance(j, int) and j < 0:
        return
    eng.wait_ge(stage.sem, j + 1 + Stage.AHEAD)


def build(nc, x, wq, wk, wv, proj, w1, b1, w2, b2, wg, bg, out):
    f32, bf16, i32 = mybir.dt.float32, mybir.dt.bfloat16, mybir.dt.int32
    ALU, ACT, AX = mybir.AluOpType, mybir.ActivationFunctionType, mybir.AxisListType

    P = 128
    B, L, D = x.shape
    TOKENS = B * L
    NE, _, F = w1.shape
    R = proj.shape[1]
    NC = F // P
    T0 = TOKENS // P
    T1 = T0 + NE - 1
    GS0, GS1 = 4, 5
    NG0, NG1 = T0 // GS0, T1 // GS1
    U = 4
    EW = F + NC
    WG = 96
    EPS_LN, EPS_Z = 1e-5, 1e-8
    FAR = 2 * TOKENS
    BANK = 512
    assert D == P and T1 % GS1 == 0 and T0 % GS0 == 0 and B == 2 and B * R <= P

    x_rows = x.rearrange("b l d -> (b l) d").rearrange("(p t) d -> p t d", t=T0)
    out_rows = out.rearrange("b l d -> (b l) d")
    RW0, RW1 = 2 * D, 2 * D + 1
    rows0 = nc.dram_tensor("rows0", (TOKENS, RW0), f32, kind="Internal").ap()
    rows1 = nc.dram_tensor("rows1", (P * T1 + 1, RW1), f32, kind="Internal").ap()
    rows0_v = rows0.rearrange("(p t) c -> p t c", t=T0)
    rows1_v = rows1[0:P * T1, :].rearrange("(p t) c -> p t c", t=T1)

    with ExitStack() as ctx:
        def sb(name, shape, dt=f32):
            return ctx.enter_context(nc.sbuf_tensor(name, shape, dt))

        def pair(name, shape, dt=f32, n=2):
            return [sb(f"{name}{i}", shape, dt) for i in range(n)]

        def sem(name):
            return ctx.enter_context(nc.semaphore(name))

        def stages(prefix, names):
            return {n: Stage(sem(f"s_{prefix}_{n}")) for n in names.split()}

        W1 = sb("W1", [P, NE * EW])
        W2 = sb("W2", [P, NE * EW])
        B2 = sb("B2", [P, NE * EW])
        B1r = sb("B1r", [NE * NC, P])
        Wg = sb("Wg", [P, WG])
        Bg = sb("Bg", [P, NE])
        Wq = sb("Wq", [P, D])
        Wk = sb("Wk", [P, D])
        Wv = sb("Wv", [P, D])
        Pr = sb("Pr", [P, R])
        Wkq = sb("Wkq", [P, 2 * R])
        WvT = sb("WvT", [P, D])
        ident = sb("ident", [P, P])
        below = sb("below", [P, P])
        below_b = sb("below_b", [P, P], bf16)
        ones_b = sb("ones_b", [P, P], bf16)
        zeros = sb("zeros", [P, NE * T1])
        neghalf = sb("neghalf", [P, T1])
        lane_i = sb("lane_i", [P, P], i32)
        lane_b = sb("lane_b", [P, P], bf16)
        lane_f = sb("lane_f", [P, T1])
        part_i = sb("part_i", [P, 1], i32)
        part1 = sb("part1", [P, 1])
        exp_no_i = sb("exp_no_i", [P, NE, T1], i32)
        exp_no = sb("exp_no", [P, NE, T1])
        padrow = sb("padrow", [1, RW1])
        warm = sb("warm", [P, 1])

        X0 = sb("X0", [P, T0, D])
        X1 = sb("X1", [P, T1, D + 1])
        STATS = sb("STATS", [P, T1, 6])
        MR = sb("MR", [P, T1, 2])
        VE = sb("VE", [P, T1])
        QT = sb("QT", [B * R, T1 * P])
        DEN = sb("DEN", [P, T1])
        DENE = sb("DENE", [P, T1])
        Z = sb("Z", [P, T1])
        batch = sb("batch", [P, T1, B])
        xn = pair("xn", [P, GS1, D])
        XN = sb("XN", [P, T1, D])
        xnT = pair("xnT", [P, GS1 * P])
        stats = pair("stats", [P, GS1, 6])
        mv = pair("mv", [P, GS1, 2])
        mr = pair("mr", [P, GS1, 2])
        ve = pair("ve", [P, GS1])
        rstd = pair("rstd", [P, GS1])
        nmean = pair("nmean", [P, GS1])
        nmr = pair("nmr", [P, GS1])
        expo = pair("expo", [P, GS1, 2 * R])
        relu = pair("relu", [P, GS1, 2 * R])
        feat = pair("feat", [P, GS1, 2 * R])
        kmask = pair("kmask", [P, GS1, B * R])
        qmask = pair("qmask", [P, GS1, B * R])
        qs = pair("qs", [B * R, GS1 * P])
        G = sb("G", [B * R, D])
        GT = sb("GT", [P, B * R])
        KV = sb("KV", [B * R, D])

        lg = sb("lg", [P, NE, T1])
        hot_b = sb("hot_b", [P, NE * T1], bf16)
        cum = sb("cum", [P, NE * T1])
        AV = sb("AV", [P, T1, 3, T1], bf16)
        SL = sb("SL", [P, T1, P], bf16)
        cnt_i, til_i = sb("cnt_i", [P, NE], i32), sb("til_i", [P, NE], i32)
        ends = sb("ends", [P, NE + 1])
        cnt, til, tend, tstart, base = (sb(n, [P, NE]) for n in ("cnt", "til", "tend", "tstart", "base"))
        eq, pref, hot, hot2, where, where2, where3 = (
            sb(n, [P, NE, T1]) for n in ("eq", "pref", "hot", "hot2", "where", "where2", "where3"))
        top, first, filled, pos, posx, tile_f, gsum, ra, rb, rc, rd, empty = (
            sb(n, [P, T1]) for n in ("top", "first", "filled", "pos", "posx", "tile_f", "gsum", "ra", "rb", "rc", "rd",
                                     "empty"))
        pos_i, tile_i, slot_i = (sb(n, [P, T1], i32) for n in ("pos_i", "tile_i", "slot_i"))
        slot_b = sb("slot_b", [P, T1], bf16)
        ge = sb("ge", [P, NE - 1, T1])
        tab = sb("tab", [P, 2, T1])
        expert = pair("expert", [P, T1 + U], i32)
        src = pair("src", [P, T1 + U], i32)


        g_in = pair("g_in", [P, RW1], n=U)
        g_idx = pair("g_idx", [P, 1], i32, n=U)
        token = pair("token", [P, 1], i32, n=U)
        o_idx = pair("o_idx", [P, 1], i32, n=U)
        res = pair("res", [P, D], n=U)
        o_out = pair("o_out", [P, D], n=U)
        hT_in = pair("hT_in", [P, P])
        w1e = pair("w1e", [P, EW], n=U)
        hT = pair("hT", [P, F], n=U)

        PA, PB, PC, PD = (ctx.enter_context(nc.psum_tensor(n, [P, 2 * BANK], f32)) for n in ("PA", "PB", "PC", "PD"))

        def bank(area, i, n):
            return area[:, BANK * i:BANK * i + n]
        PA_BANKS = [bank(PA, i, BANK) for i in range(2)]

        s_w = {n: sem("s_w_" + n) for n in ("w1", "w2", "b1", "b2", "wg", "bg", "wq", "wk", "wv", "pr")}
        HALF = T0 // 2
        s_xload = [sem(f"s_xload{i}") for i in range(2)]
        s_rows0x = sem("s_rows0x")
        s_rows0n = [sem(f"s_rows0n{i}") for i in range(2)]
        s_rows1x = sem("s_rows1x")
        s_rows1n = [sem(f"s_rows1n{i}") for i in range(2)]
        s_XN = [sem(f"s_XN{i}") for i in range(2)]
        s_padrow = sem("s_padrow")
        s_const = sem("s_const")
        s_constd = sem("s_constd")
        s_fold = sem("s_fold")
        s_foldd = sem("s_foldd")
        s_warm = sem("s_warm")
        s_ln = [sem(f"s_ln{i}") for i in range(2)]
        s_pow = [sem(f"s_pow{i}") for i in range(2)]
        s_qs = [sem(f"s_qs{i}") for i in range(2)]
        s_mid = sem("s_mid")
        s_midd = sem("s_midd")
        s_alone = {e.engine: sem(f"s_alone{n}")
                   for n, e in enumerate((nc.gpsimd, nc.vector, nc.tensor, nc.scalar, nc.sync))}
        s_rd = [sem(f"s_route_dve{f}") for f in range(2)]
        s_rp = [sem(f"s_route_pe{f}") for f in range(2)]
        s_rpool = [sem(f"s_route_pool{f}") for f in range(2)]
        l0 = stages("l0", "mr xn xT xTs mm lg")
        la = stages("la", "mr xn xT xTs mm kx feat km qm den gt qt qts")
        lb = stages("lb", "num x2 stat mean ve rstd nm nmr xn xT xTs mm lg")
        ffn = [stages(f"f{i}", "xT xTs w1e up hT res down out") for i in range(2)]
        s_idx = [sem(f"s_idx{i}") for i in range(2)]
        s_st = sem("s_st")
        s_gather = [[sem(f"s_gather{f}_{i}") for i in range(U)] for f in range(2)]
        s_scatter = [sem(f"s_scatter_{i}") for i in range(U)]

        block = ctx.enter_context(nc.Block())

        def alone(eng):
            eng.sem_inc(s_alone[eng.engine])

        def row(a, t, n=D):
            return a[:, bass.ds(t, 1), 0:n].rearrange("p a d -> p (a d)")


        def ln_variance(eng, f, piece, lo, hi):
            n = LN_STEPS * piece

            def did(i, wait=True):
                nonlocal n
                i.then_inc(s_ln[f], 1)
                n += 1
                if wait:
                    eng.wait_ge(s_ln[f], n)
            did(eng.tensor_tensor(ra[:, lo:hi], STATS[:, lo:hi, 1], STATS[:, lo:hi, 4], ALU.add), False)
            did(eng.tensor_tensor(rb[:, lo:hi], STATS[:, lo:hi, 1], STATS[:, lo:hi, 4], ALU.subtract), False)
            did(eng.tensor_tensor(rc[:, lo:hi], STATS[:, lo:hi, 2], STATS[:, lo:hi, 5], ALU.add))
            did(eng.tensor_scalar(MR[:, lo:hi, 0], ra[:, lo:hi], 0.5, None, ALU.mult), False)
            did(eng.tensor_tensor(rd[:, lo:hi], rb[:, lo:hi], rb[:, lo:hi], ALU.mult), False)
            did(eng.tensor_scalar(gsum[:, lo:hi], rc[:, lo:hi], 1.0 / D, EPS_LN, ALU.mult, ALU.add))
            did(eng.scalar_tensor_tensor(out=VE[:, lo:hi], in0=rd[:, lo:hi], scalar=0.25, in1=gsum[:, lo:hi],
                                         op0=ALU.mult, op1=ALU.add), False)
        LN_STEPS = 7
        EARLY = (T1 - 4) // GS1

        def ln_rstd(eng, f, piece, gs, g0, g1):
            eng.wait_ge(s_ln[f], LN_STEPS * (piece + 1))
            for g in range(g0, g1):
                eng.tensor_tensor(MR[:, g * gs:(g + 1) * gs, 1], VE[:, g * gs:(g + 1) * gs], neghalf[:, 0:gs], ALU.pow)\
                   .then_inc(s_pow[f], 1)

        def ln_mr(eng, f, s, gs, st):
            eng.wait_ge(s_pow[f], st.j + 1)
            need(eng, s["xn"], st.j - 2)
            s["mr"].done(eng.tensor_copy(mr[st.k][:, 0:gs, :], MR[:, bass.ds(st.j * gs, gs), :]))

        def xn_free(eng, s, s_copied, st):
            need(eng, s["xT"], st.j - 2)
            if not (isinstance(st.j, int) and st.j < 2):
                eng.wait_ge(s_copied[st.k], st.turns16)

        def ln_norm(eng, X, s, s_copied, gs, st):
            k = st.k
            xn_free(eng, s, s_copied, st)
            need(eng, s["mr"], st.j)
            alone(eng)
            for t in range(gs):
                i = eng.tensor_scalar(xn[k][:, t, :], row(X, st.j * gs + t), mr[k][:, t, 0:1], mr[k][:, t, 1:2],
                                      ALU.subtract, ALU.mult)
            s["xn"].done(i)

        def ln_turn(eng, s, gs, areas, st):
            area = areas[st.k % len(areas)]
            need(eng, s["xn"], st.j)
            need(eng, s["xTs"], st.j - len(areas))
            alone(eng)
            for t in range(gs):
                i = eng.transpose(area[:, t * P:(t + 1) * P], xn[st.k][:, t, :], ident[:, :])
            s["xT"].done(i)

        def ln_copy(eng, s, gs, areas, st):
            area = areas[st.k % len(areas)]
            need(eng, s["xT"], st.j)
            need(eng, s["mm"], st.j - 2)
            s["xTs"].done(eng.activation(xnT[st.k][:, 0:gs * P], area[:, 0:gs * P], ACT.Copy))

        def gate_mm(eng, s, gs, st):
            need(eng, s["xTs"], st.j)
            need(eng, s["lg"], st.j - 2)
            for t in range(gs):
                i = eng.matmul(PB[:, BANK * st.k + t * WG:BANK * st.k + (t + 1) * WG], xnT[st.k][:, t * P:(t + 1) * P],
                               Wg[:, :], start=True, stop=True)
            s["mm"].done(i)

        def gate_add(eng, s, gs, st):
            need(eng, s["mm"], st.j)
            s["lg"].done(eng.tensor_tensor(lg[:, :, bass.ds(st.j * gs, gs)],
                                           bank(PB, st.k, gs * WG).rearrange("p (t e) -> p e t", e=WG)[:, 0:NE, :],
                                           Bg[:, :].unsqueeze(2).to_broadcast([P, NE, gs]), ALU.add))

        SPLIT = 7
        AT = [{}, {}]

        def te(a, T):
            return a[:, :, 0:T].rearrange("p e t -> p t e")

        def wide(a, T):
            return a[:, 0:T].unsqueeze(2).to_broadcast([P, T, T1])

        def route_pool(eng, f):
            T = (T0, T1)[f]
            eng.wait_ge(s_rd[f], AT[f]["tile"])
            eng.tensor_tensor(AV[:, 0:T, 2, :], AV[:, 0:T, 0, :], wide(lane_f, T), ALU.mult).then_inc(s_rpool[f], 1)

        def route_dve(eng, f):
            T, n, at = (T0, T1)[f], [0], AT[f]

            def did(i, chain=True):
                i.then_inc(s_rd[f], 1)
                n[0] += 1
                if chain:
                    eng.wait_ge(s_rd[f], n[0])

            def reached(name):
                assert at[name] == n[0], (name, n[0])

            def first_rows():
                for j in range(U):
                    eng.tensor_copy(g_idx[j][:, :], src[f][:, j:j + 1]).then_inc(s_idx[f], 1)

            def over_e(a):
                return a[:, 0:T].unsqueeze(1).to_broadcast([P, NE, T])

            need(eng, (l0, lb)[f]["lg"], (NG0, NG1)[f] - 1)
            did(eng.tensor_reduce(top[:, 0:T], te(lg, T), AX.X, ALU.max))
            did(eng.tensor_tensor(eq[:, :, 0:T], lg[:, :, 0:T], over_e(top), ALU.is_ge))
            did(eng.scalar_tensor_tensor(out=pref[:, :, 0:T], in0=eq[:, :, 0:T], scalar=-8.0, in1=exp_no[:, :, 0:T],
                                         op0=ALU.mult, op1=ALU.add))
            did(eng.tensor_reduce(first[:, 0:T], te(pref, T), AX.X, ALU.min))
            did(eng.tensor_tensor(hot[:, :, 0:T], pref[:, :, 0:T], over_e(first), ALU.is_equal))
            h = hot
            if f:
                did(eng.tensor_tensor(hot2[:, :, :], hot[:, :, :], over_e(filled), ALU.mult))
                h = hot2
            did(eng.tensor_copy(hot_b[:, 0:NE * T].rearrange("p (e t) -> p e t", e=NE), h[:, :, 0:T]))
            reached("hot")
            did(eng.memset(ends[:, 0:1], 0.0), False)
            eng.wait_ge(s_rp[f], 1)
            did(eng.tensor_tensor_scan(cum[:, 0:NE * T], PC[:, 0:NE * T], zeros[:, 0:NE * T], 0.0, ALU.add, ALU.add))
            c3 = cum[:, 0:NE * T].rearrange("p (e t) -> p e t", e=NE)
            did(eng.tensor_copy(ends[:, 1:NE + 1], c3[:, :, T - 1]))
            did(eng.tensor_tensor(cnt[:, :], ends[:, 1:NE + 1], ends[:, 0:NE], ALU.subtract))
            did(eng.tensor_scalar(cnt_i[:, :], cnt[:, :], float(P - 1), None, ALU.add))
            did(eng.tensor_scalar(til_i[:, :], cnt_i[:, :], 7, None, ALU.arith_shift_right))
            did(eng.tensor_copy(til[:, :], til_i[:, :]))
            did(eng.tensor_tensor_scan(tend[:, :], til[:, :], zeros[:, 0:NE], 0.0, ALU.add, ALU.add))
            did(eng.tensor_tensor(tstart[:, :], tend[:, :], til[:, :], ALU.subtract))
            did(eng.scalar_tensor_tensor(out=base[:, :], in0=tstart[:, :], scalar=float(P), in1=ends[:, 0:NE],
                                         op0=ALU.mult, op1=ALU.subtract))
            did(eng.tensor_tensor(where[:, :, 0:T], c3, base[:, :].unsqueeze(2).to_broadcast([P, NE, T]), ALU.add))
            did(eng.tensor_tensor(where2[:, :, 0:T], where[:, :, 0:T],
                                  bank(PC, 1, NE * T).rearrange("p (e t) -> p e t", e=NE), ALU.add))
            did(eng.tensor_tensor(where3[:, :, 0:T], where2[:, :, 0:T], h[:, :, 0:T], ALU.mult))
            did(eng.tensor_reduce(pos[:, 0:T], te(where3, T), AX.X, ALU.add))
            p_ = pos
            if f:
                did(eng.scalar_tensor_tensor(out=posx[:, :], in0=empty[:, :], scalar=float(FAR), in1=pos[:, :],
                                             op0=ALU.mult, op1=ALU.add))
                p_ = posx
            did(eng.tensor_copy(pos_i[:, 0:T], p_[:, 0:T]))
            did(eng.tensor_scalar(tile_i[:, 0:T], pos_i[:, 0:T], 7, None, ALU.arith_shift_right), False)
            did(eng.tensor_scalar(slot_i[:, 0:T], pos_i[:, 0:T], P - 1, None, ALU.bitwise_and))
            did(eng.tensor_copy(tile_f[:, 0:T], tile_i[:, 0:T]), False)
            did(eng.tensor_copy(slot_b[:, 0:T], slot_i[:, 0:T]))
            a1 = AV[:, 0:T, 0, :]
            did(eng.tensor_tensor(a1, wide(tile_f, T), lane_f[:, :].unsqueeze(1).to_broadcast([P, T, T1]),
                                  ALU.is_equal))
            reached("tile")
            did(eng.tensor_scalar(AV[:, 0:T, 1, :], a1, part1[:, 0:1], None, ALU.mult), False)
            for c in range(0, T, SPLIT):
                w = min(SPLIT, T - c)
                did(eng.tensor_tensor(SL[:, c:c + w, :], slot_b[:, c:c + w].unsqueeze(2).to_broadcast([P, w, P]),
                                      lane_b[:, :].unsqueeze(1).to_broadcast([P, w, P]), ALU.is_equal), False)
                reached(f"slots{c // SPLIT}")
            for e in range(1, NE):
                did(eng.tensor_scalar(ge[:, e - 1, :], lane_f[:, :], tstart[:, e:e + 1], float(EW), ALU.is_ge, ALU.mult),
                    e == NE - 1)
            did(eng.tensor_tensor(gsum[:, :], ge[:, 0, :], ge[:, 1, :], ALU.add))
            did(eng.tensor_tensor(expert[f][:, 0:T1], gsum[:, :], ge[:, 2, :], ALU.add), False)
            eng.wait_ge(s_rp[f], 2)
            did(eng.tensor_copy(tab[:, :, :], PC[:, 0:2 * T1].rearrange("p (c t) -> p c t", t=T1)))
            did(eng.tensor_scalar(ra[:, :], tab[:, 0, :], -1.0, float(T), ALU.add, ALU.mult), False)
            did(eng.tensor_scalar(empty[:, :] if f == 0 else rd[:, :], tab[:, 0, :], 0.0, None, ALU.is_equal))
            if f == 0:
                did(eng.tensor_tensor(rb[:, :], ra[:, :], tab[:, 1, :], ALU.add))
                did(eng.tensor_scalar(src[0][:, 0:T1], rb[:, :], 0.0, None, ALU.max))
                reached("done")
                first_rows()
                did(eng.scalar_tensor_tensor(out=rc[:, :], in0=empty[:, :], scalar=float(FAR), in1=rb[:, :],
                                             op0=ALU.mult, op1=ALU.add), False)
                did(eng.tensor_scalar(filled[:, :], empty[:, :], -1.0, 1.0, ALU.mult, ALU.add), False)
                did(eng.tensor_scalar(batch[:, :, 1], tab[:, 0, :], float(P // B + 1), None, ALU.is_ge))
                did(eng.tensor_copy(X1[:, :, D:D + 1].bitcast(i32).rearrange("p t a -> p (t a)"), rc[:, :]), False)
                did(eng.tensor_tensor(batch[:, :, 0], filled[:, :], batch[:, :, 1], ALU.subtract))
            else:
                did(eng.tensor_tensor(rb[:, :], ra[:, :], tab[:, 1, :], ALU.add), False)
                did(eng.tensor_scalar(rc[:, :], rd[:, :], float((P + 1) * T1), None, ALU.mult))
                did(eng.tensor_tensor(src[1][:, 0:T1], rb[:, :], rc[:, :], ALU.add))
                reached("done")
                first_rows()

        def route_counts():
            for f, T in enumerate((T0, T1)):
                c = AT[f]
                c["hot"] = 6 + f
                c["tile"] = c["hot"] + 1 + 13 + f + 5 + 1
                slots = c["tile"] + 1
                for i in range(-(-T // SPLIT)):
                    c[f"slots{i}"] = slots + i + 1
                c["done"] = slots + -(-T // SPLIT) + (NE - 1) + 2 + 3 + (2 if f == 0 else 3)
        route_counts()

        def route_pe(eng, f):
            T = (T0, T1)[f]
            eng.wait_ge(s_rd[f], AT[f]["hot"])
            eng.matmul(PC[:, 0:NE * T], ones_b[:, :], hot_b[:, 0:NE * T], start=True, stop=True)
            eng.matmul(PC[:, BANK:BANK + NE * T], below_b[:, :], hot_b[:, 0:NE * T], start=True, stop=True)\
               .then_inc(s_rp[f], 1)
            eng.wait_ge(s_rpool[f], 1)
            for t in range(T):
                if t % SPLIT == 0:
                    eng.wait_ge(s_rd[f], AT[f][f"slots{t // SPLIT}"])
                i = eng.matmul(PC[:, 0:2 * T1], SL[:, t, :], AV[:, t, 1:3, :].rearrange("p c t -> p (c t)"),
                               start=(t == 0), stop=(t == T - 1))
            i.then_inc(s_rp[f], 1)


        def ffn_pool(eng, f):
            s, rows, RW = ffn[f], (rows0, rows1)[f], (RW0, RW1)[f]
            eng.wait_ge(s_rd[f], AT[f]["done"])
            if f == 0:
                eng.wait_ge(s_rows0x, 16)
                for k in range(2):
                    eng.wait_ge(s_rows0n[k], 16 * (NG0 // 2))
            else:
                eng.wait_ge(s_padrow, 16)
                eng.wait_ge(s_rows1x, 16 * NG1)
                for k in range(2):
                    eng.wait_ge(s_rows1n[k], 16 * ((NG1 + 1 - k) // 2))

            def gather(st):
                k = st.k
                need(eng, s["res"], st.j - U)
                alone(eng)
                eng.indirect_dma_start(out=g_in[k][:, 0:RW], out_offset=None, in_=rows,
                                       in_offset=bass.IndirectOffsetOnAxis(ap=g_idx[k][:, 0:1], axis=0))\
                   .then_inc(s_gather[f][k], 16)

            def scatter(st):
                k = st.k
                need(eng, s["out"], st.j)
                alone(eng)
                eng.indirect_dma_start(out=out_rows, out_offset=bass.IndirectOffsetOnAxis(ap=o_idx[k][:, 0:1], axis=0),
                                       in_=o_out[k][:, :], in_offset=None,
                                       bounds_check=TOKENS - 1, oob_is_err=False).then_inc(s_scatter[k], 16)

            eng.wait_ge(s_idx[f], U)
            if f == 0:
                run_steps(eng, U, T1 - T1 % U, T1, U, lambda st, _: gather(st))
                return
            LEAD = U + 2
            for j in range(LEAD):
                gather(step_of(j, U))

            def both(st, _):
                if st.at_most(T1 - 1 - LEAD):
                    gather(st.plus(LEAD))
                scatter(st)
            last = T1 - T1 % U - U
            run_steps(eng, U, last, T1, U, both)
            for k in range(U):
                eng.wait_ge(s_scatter[k], 16 * ((T1 - k + U - 1) // U))

        def experts_of(eng, f, j, n):
            _, values = nc.values_load_multi_w_load_instructions(
                expert[f][0:1, bass.ds(j, n)], engines=[eng.engine], min_val=0, max_val=(NE - 1) * EW,
                skip_runtime_bounds_check_because="DVE sums at most NE-1 comparisons times EW")
            return values

        def ffn_pe(eng, f):
            s = ffn[f]
            ln_at = (RW0, RW1)[f] - D
            if f == 0:
                eng.wait_ge(s_w["w1"], 16)
                eng.wait_ge(s_w["w2"], 16 * NE)
            eng.wait_ge(s_rd[f], AT[f]["done"])

            def turn_in(st):
                eng.wait_ge(s_gather[f][st.k], st.turns16 + 16)
                s["xT"].done(eng.transpose(bank(PD, st.k % 2, P), g_in[st.k][:, ln_at:ln_at + D], ident[:, :]))

            def up(st):
                need(eng, s["xTs"], st.j)
                need(eng, s["w1e"], st.j)
                for c in range(NC):
                    i = eng.matmul(PA[:, BANK * (st.k % 2) + c * P:BANK * (st.k % 2) + (c + 1) * P],
                                   w1e[st.k][:, c * P:(c + 1) * P], hT_in[st.k % 2][:, :], start=True, stop=True)
                s["up"].done(i)

            def down(st, e):
                need(eng, s["hT"], st.j)
                if isinstance(st.j, int):
                    need(eng, s["out"], st.j - 2)
                for c in range(NC):
                    i = eng.matmul(bank(PC, st.k % 2, D), hT[st.k][:, c * P:(c + 1) * P], W2[:, bass.ds(e + c * P, D)],
                                   start=(c == 0), stop=(c == NC - 1))
                s["down"].done(i)

            def load(j):
                return experts_of(eng, f, j, min(U, T1 - j) if isinstance(j, int) else U)
            turn_in(step_of(0, U))
            turn_in(step_of(1, U))
            up(step_of(0, U))
            turn_in(step_of(2, U))
            up(step_of(1, U))

            def body(st, e):
                if st.at_most(T1 - 4):
                    turn_in(st.plus(3))
                if st.at_most(T1 - 3):
                    up(st.plus(2))
                down(st, e[st.k])
            run_steps(eng, U, T1 - 3, T1, U, body, load)

        def ffn_act(eng, f):
            s = ffn[f]

            def copy_in(st):
                need(eng, s["xT"], st.j)
                s["xTs"].done(eng.activation(hT_in[st.k % 2][:, :], bank(PD, st.k % 2, P), ACT.Copy))

            def gelu(st):
                need(eng, s["up"], st.j)
                for c in range(NC):
                    i = eng.activation(hT[st.k][:, c * P:(c + 1) * P],
                                       PA[:, BANK * (st.k % 2) + c * P:BANK * (st.k % 2) + (c + 1) * P], ACT.Gelu,
                                       bias=w1e[st.k][:, F + c:F + c + 1])
                s["hT"].done(i)
            copy_in(step_of(0, U))
            copy_in(step_of(1, U))
            gelu(step_of(0, U))
            copy_in(step_of(2, U))
            gelu(step_of(1, U))

            def body(st, _):
                if st.at_most(T1 - 4):
                    copy_in(st.plus(3))
                if st.at_most(T1 - 3):
                    gelu(st.plus(2))
            run_steps(eng, U, T1 - 3, T1, U, body)

        def ffn_dve(eng, f):
            s = ffn[f]

            def weights(st, e):
                s["w1e"].done(eng.tensor_copy(w1e[st.k][:, :], W1[:, bass.ds(e, EW)]))

            def residual(st, e):
                need(eng, s["out"], st.j - U)
                alone(eng)
                if f:
                    eng.tensor_copy(token[st.k][:, :], g_in[st.k][:, D:D + 1].bitcast(i32))
                eng.tensor_copy(g_idx[st.k][:, :], src[f][:, bass.ds(st.j + U, 1)])
                s["res"].done(eng.tensor_tensor(res[st.k][:, :], g_in[st.k][:, 0:D], B2[:, bass.ds(e, D)], ALU.add))

            def finish(st):
                need(eng, s["down"], st.j)
                need(eng, s["res"], st.j)
                alone(eng)
                if f and not (isinstance(st.j, int) and st.j < U):
                    eng.wait_ge(s_scatter[st.k], st.turns16)
                if f:
                    eng.tensor_copy(o_idx[st.k][:, :], token[st.k][:, :])
                s["out"].done(eng.scalar_tensor_tensor(out=row(X1, st.j) if f == 0 else o_out[st.k][:, :],
                                                       in0=bank(PC, st.k % 2, D), scalar=0.5, in1=res[st.k][:, :],
                                                       op0=ALU.mult, op1=ALU.add))

            def stat(j):
                need(eng, s["out"], j)
                alone(eng)
                eng.bn_stats(row(STATS, j, 6), row(X1, j)).then_inc(s_st, 1)

            def load(j):
                n = U + 1 if not isinstance(j, int) else min(U + 1, T1 - 3 - j)
                return experts_of(eng, f, j + 3, n) if n > 0 else None
            e0 = experts_of(eng, f, 0, U)
            for j in range(U):
                weights(step_of(j, U), e0[j])
            for j in range(3):
                need(eng, s["xT"], j)
                residual(step_of(j, U), e0[j])

            def body(st, e):
                finish(st)
                if st.at_most(T1 - 1 - U):
                    weights(st.plus(4), e[st.k + 1])
                if st.at_most(T1 - 4):
                    residual(st.plus(3), e[st.k])
                if f == 0 and not (isinstance(st.j, int) and st.j < 1):
                    stat(st.j - 1)

            def early_variance():
                eng.wait_ge(s_st, T0 + EARLY * GS1)
                ln_variance(eng, 1, 0, 0, EARLY * GS1)
            run_steps(eng, U, T1 - 3, T1, U, body, load, early_variance if f == 0 else None)
            if f == 0:
                stat(T1 - 1)


        def masked(eng, o, c, st):
            m = batch[:, bass.ds(st.j * GS1, GS1), :].unsqueeze(3).to_broadcast([P, GS1, B, R])
            return eng.tensor_tensor(o[st.k][:, :, :].rearrange("p t (b r) -> p t b r", b=B),
                                     feat[st.k][:, :, c:c + R].unsqueeze(2).to_broadcast([P, GS1, B, R]), m, ALU.mult)

        def la_features(eng, st):
            k = st.k
            need(eng, la["kx"], st.j)
            need(eng, la["qm"], st.j - 2)
            la["feat"].done(eng.scalar_tensor_tensor(out=feat[k][:, :, :], in0=expo[k][:, :, :], scalar=1.0,
                                                     in1=relu[k][:, :, :], op0=ALU.min, op1=ALU.add))
            need(eng, la["gt"], st.j - 2)
            need(eng, la["feat"], st.j)
            alone(eng)
            la["km"].done(masked(eng, kmask, 0, st))
            la["den"].done(eng.tensor_reduce(DEN[:, bass.ds(st.j * GS1, GS1)], feat[k][:, :, R:2 * R], AX.X, ALU.add))

        def la_query_mask(eng, st):
            need(eng, la["feat"], st.j)
            need(eng, la["qt"], st.j - 2)
            alone(eng)
            la["qm"].done(masked(eng, qmask, R, st))

        def keep_xn(st):
            need(nc.sync, la["xn"], st.j)
            alone(nc.sync)
            nc.sync.dma_start(XN[:, bass.ds(st.j * GS1, GS1), :], xn[st.k][:, :, :]).then_inc(s_XN[st.k], 16)

        def la_sum(eng, st):
            k = st.k
            need(eng, la["km"], st.j)
            eng.wait_ge(s_XN[k], st.turns16 + 16)
            alone(eng)
            for t in range(GS1):
                i = eng.matmul(PC[0:B * R, 0:D], kmask[k][:, t, :], row(XN, st.j * GS1 + t),
                               start=False, stop=isinstance(st.j, int) and st.j == NG1 - 1 and t == GS1 - 1)
            la["gt"].done(i)
            need(eng, la["qm"], st.j)
            need(eng, la["qts"], st.j - 1)
            alone(eng)
            for t in range(GS1):
                i = eng.transpose(PD[0:B * R, t * P:(t + 1) * P], qmask[k][:, t, :], ident[:, :])
            la["qt"].done(i)

        def la_mm(eng, st):
            need(eng, la["xTs"], st.j)
            need(eng, la["kx"], st.j - 2)
            for t in range(GS1):
                i = eng.matmul(PB[:, BANK * st.k + t * 2 * R:BANK * st.k + (t + 1) * 2 * R],
                               xnT[st.k][:, t * P:(t + 1) * P], Wkq[:, :], start=True, stop=True)
            la["mm"].done(i)

        def la_act_q(eng, st):
            need(eng, la["qt"], st.j)
            alone(eng)
            la["qts"].done(eng.activation(QT[:, bass.ds(st.j * (GS1 * P), GS1 * P)], PD[0:B * R, 0:GS1 * P], ACT.Copy))

        def la_act_exp(eng, st):
            k = st.k
            need(eng, la["mm"], st.j)
            need(eng, la["feat"], st.j - 2)
            v = bank(PB, k, GS1 * 2 * R)
            eng.activation(relu[k][:, :, :].rearrange("p t c -> p (t c)"), v, ACT.Relu)
            la["kx"].done(eng.activation(expo[k][:, :, :].rearrange("p t c -> p (t c)"), v, ACT.Exp))


        def lb_queries(eng, st):
            need(eng, la["qts"], st.j)
            alone(eng)
            need(eng, lb["num"], st.j - 2)
            alone(eng)
            eng.dma_start(qs[st.k][:, :], QT[:, bass.ds(st.j * (GS1 * P), GS1 * P)]).then_inc(s_qs[st.k], 16)

        def lb_rstd(eng, st):
            k = st.k
            need(eng, lb["mean"], st.j)
            need(eng, lb["xn"], st.j - 2)
            alone(eng)
            lb["ve"].done(eng.tensor_scalar(ve[k][:, :], mv[k][:, :, 1], EPS_LN, None, ALU.add))
            lb["nm"].done(eng.tensor_scalar(nmean[k][:, :], mv[k][:, :, 0], -1.0, None, ALU.mult))
            need(eng, lb["ve"], st.j)
            lb["rstd"].done(eng.tensor_tensor(rstd[k][:, :], ve[k][:, :], neghalf[:, 0:GS1], ALU.pow))
            need(eng, lb["nm"], st.j)
            need(eng, lb["rstd"], st.j)
            lb["nmr"].done(eng.tensor_tensor(nmr[k][:, :], nmean[k][:, :], rstd[k][:, :], ALU.mult))

        def lb_num(eng, st):
            eng.wait_ge(s_qs[st.k], st.turns16 + 16)
            need(eng, lb["x2"], st.j - 2)
            alone(eng)
            for t in range(GS1):
                i = eng.matmul((PC, PD)[st.k][:, t * P:(t + 1) * P], qs[st.k][:, t * P:(t + 1) * P], KV[:, :],
                               start=True, stop=True)
            lb["num"].done(i)

        def lb_x2(eng, st):
            k = st.k
            need(eng, lb["num"], st.j)
            for t in range(GS1):
                xt = row(X1, st.j * GS1 + t)
                i = eng.scalar_tensor_tensor(out=xt, in0=(PC, PD)[k][:, t * P:(t + 1) * P], scalar=Z[:, bass.ds(st.j * GS1 + t, 1)],
                                             in1=xt, op0=ALU.mult, op1=ALU.add)
            lb["x2"].done(i)
            need(eng, lb["x2"], st.j)
            alone(eng)
            for t in range(GS1):
                i = eng.bn_stats(stats[k][:, t, :], row(X1, st.j * GS1 + t))
            lb["stat"].done(i)
            need(eng, lb["nmr"], st.j - 2)
            need(eng, lb["stat"], st.j)
            alone(eng)
            for t in range(GS1):
                i = eng.bn_aggr(mv[k][:, t, :], stats[k][:, t, :])
            lb["mean"].done(i)

        def lb_norm(eng, st):
            k = st.k
            need(eng, lb["nmr"], st.j)
            xn_free(eng, lb, s_rows1n, st)
            alone(eng)
            for t in range(GS1):
                i = eng.activation(xn[k][:, t, :], row(X1, st.j * GS1 + t), ACT.Identity,
                                   bias=nmr[k][:, t:t + 1], scale=rstd[k][:, t:t + 1])
            lb["xn"].done(i)


        def ahead(eng, s, names):
            for n in names.split():
                for _ in range(Stage.AHEAD):
                    eng.sem_inc(s[n].sem)

        @block.sync
        def _(eng):
            for i in range(2):
                eng.dma_start(X0[:, i * HALF:(i + 1) * HALF, :], x_rows[:, i * HALF:(i + 1) * HALF, :])\
                   .then_inc(s_xload[i], 16)
            eng.wait_ge(s_const, 5)
            eng.dma_start(Wg[:, 0:NE], wg).then_inc(s_w["wg"], 16)
            eng.dma_start(Bg[:, :], bg.unsqueeze(0).to_broadcast([P, NE])).then_inc(s_w["bg"], 16)
            for n, t, a in (("wq", Wq, wq), ("wk", Wk, wk), ("wv", Wv, wv), ("pr", Pr, proj)):
                eng.dma_start(t[:, :], a).then_inc(s_w[n], 16)
            eng.dma_start(B1r[:, :], b1.rearrange("e (c p) -> (e c) p", p=P)).then_inc(s_w["b1"], 16)
            for i in range(2):
                eng.wait_ge(s_xload[i], 16)

            def store0(st):
                need(eng, l0["xn"], st.j)
                alone(eng)
                eng.dma_start(rows0_v[:, bass.ds(st.j * GS0, GS0), D:2 * D], xn[st.k][:, 0:GS0, :])\
                   .then_inc(s_rows0n[st.k], 16)
            run_groups(eng, NG0, [(0, store0)])
            eng.dma_start(rows0_v[:, :, 0:D], X0[:, :, :]).then_inc(s_rows0x, 16)
            eng.wait_ge(s_const, 10)
            eng.dma_start(rows1[P * T1:P * T1 + 1, :], padrow[:, :]).then_inc(s_padrow, 16)

            def store1x(st):
                need(eng, lb["x2"], st.j)
                alone(eng)
                eng.dma_start(rows1_v[:, bass.ds(st.j * GS1, GS1), 0:D + 1], X1[:, bass.ds(st.j * GS1, GS1), :])\
                   .then_inc(s_rows1x, 16)

            def store1n(st):
                need(eng, lb["xn"], st.j)
                alone(eng)
                eng.dma_start(rows1_v[:, bass.ds(st.j * GS1, GS1), D + 1:RW1],
                              xn[st.k][:, :, :]).then_inc(s_rows1n[st.k], 16)
            run_groups(eng, NG1, [(0, keep_xn)])
            run_groups(eng, NG1, [(0, lambda st: lb_queries(eng, st)), (2, store1x), (3, store1n)])

        @block.gpsimd
        def _(eng):
            ahead(eng, la, "qm")
            ahead(eng, lb, "ve rstd nm nmr")
            eng.memset(ident[:, :], 0.0).then_inc(s_const, 1)
            eng.memset(below[:, :], -1.0).then_inc(s_const, 1)
            eng.memset(neghalf[:, :], -0.5).then_inc(s_const, 1)
            eng.memset(padrow[:, :], 0.0).then_inc(s_const, 1)
            eng.memset(Wg[:, :], 0.0).then_inc(s_const, 1)
            eng.wait_ge(s_const, 5)
            eng.affine_select(out=ident[:, :], in_=ident[:, :], compare_op=ALU.not_equal, fill=1.0, base=0,
                              pattern=[[-1, P]], channel_multiplier=1).then_inc(s_const, 1)
            eng.affine_select(out=below[:, :], in_=below[:, :], compare_op=ALU.is_ge, fill=0.0, base=0,
                              pattern=[[-1, P]], channel_multiplier=1).then_inc(s_const, 1)
            eng.iota(lane_i[:, :], pattern=[[1, P]], base=0, channel_multiplier=0).then_inc(s_const, 1)
            eng.iota(part_i[:, :], pattern=[[1, 1]], base=1, channel_multiplier=1).then_inc(s_const, 1)
            eng.iota(padrow[:, D:D + 1].bitcast(i32), pattern=[[0, 1]], base=FAR, channel_multiplier=0)\
               .then_inc(s_const, 1)
            eng.iota(exp_no_i[:, :, :], pattern=[[1, NE], [0, T1]], base=0, channel_multiplier=0).then_inc(s_const, 1)
            for i in range(2):
                ln_rstd(eng, 0, i, GS0, i * NG0 // 2, (i + 1) * NG0 // 2)
            route_pool(eng, 0)
            ffn_pool(eng, 0)
            ln_rstd(eng, 1, 0, GS1, 0, EARLY)
            ln_rstd(eng, 1, 1, GS1, EARLY, NG1)
            run_groups(eng, NG1, [(0, lambda st: la_query_mask(eng, st))])
            run_groups(eng, NG1, [(0, lambda st: lb_rstd(eng, st))])
            route_pool(eng, 1)
            ffn_pool(eng, 1)

        @block.vector
        def _(eng):
            ahead(eng, l0, "mr xn lg")
            ahead(eng, la, "mr xn feat km den")
            ahead(eng, lb, "x2 stat mean lg")
            for f in range(2):
                ahead(eng, ffn[f], "w1e res out")
            eng.wait_ge(s_const, 11)
            eng.memset(ones_b[:, :], 1.0).then_inc(s_constd, 1)
            eng.memset(zeros[:, :], 0.0).then_inc(s_constd, 1)
            for f in range(2):
                eng.memset(src[f][:, T1:T1 + U], 0).then_inc(s_constd, 1)
                eng.memset(expert[f][:, T1:T1 + U], 0).then_inc(s_constd, 1)
            eng.tensor_copy(below_b[:, :], below[:, :]).then_inc(s_constd, 1)
            eng.tensor_copy(lane_b[:, :], lane_i[:, :]).then_inc(s_constd, 1)
            eng.tensor_copy(lane_f[:, :], lane_i[:, 0:T1]).then_inc(s_constd, 1)
            eng.tensor_copy(part1[:, :], part_i[:, :]).then_inc(s_constd, 1)
            eng.tensor_copy(exp_no[:, :, :], exp_no_i[:, :, :]).then_inc(s_constd, 1)
            for i in range(2):
                eng.wait_ge(s_xload[i], 16)
                for t in range(i * HALF, (i + 1) * HALF):
                    eng.bn_stats(STATS[:, t, :], X0[:, t, :]).then_inc(s_st, 1)
                eng.wait_ge(s_st, (i + 1) * HALF)
                ln_variance(eng, 0, i, i * HALF, (i + 1) * HALF)
            eng.wait_ge(s_w["bg"], 16)
            run_groups(eng, NG0, [(0, lambda st: ln_mr(eng, 0, l0, GS0, st)),
                                  (1, lambda st: ln_norm(eng, X0, l0, s_rows0n, GS0, st)),
                                  (3, lambda st: gate_add(eng, l0, GS0, st))])
            route_dve(eng, 0)
            eng.wait_ge(s_w["w1"], 16)
            eng.wait_ge(s_w["b2"], 16)
            b2v = B2[:, :].rearrange("p (e f) -> p e f", e=NE)[:, :, 0:D]
            eng.tensor_scalar(b2v, b2v, 0.5, None, ALU.mult).then_inc(s_foldd, 1)
            eng.wait_ge(s_fold, 1)
            eng.tensor_copy(Wkq[:, :], PD[:, 0:2 * R]).then_inc(s_foldd, 1)
            eng.tensor_copy(WvT[:, :], PD[:, BANK:BANK + D]).then_inc(s_foldd, 1)
            eng.tensor_copy(W1[:, :].rearrange("p (e f) -> p e f", e=NE)[:, :, F:EW],
                            PD[:, 2 * R:2 * R + NE * NC].rearrange("p (e c) -> p e c", e=NE)).then_inc(s_foldd, 1)
            eng.wait_ge(s_foldd, 4)
            ffn_dve(eng, 0)
            eng.wait_ge(s_st, T0 + T1)
            ln_variance(eng, 1, 1, EARLY * GS1, T1)
            run_groups(eng, NG1, [(1, lambda st: ln_norm(eng, X1, la, s_XN, GS1, st)),
                                  (0, lambda st: ln_mr(eng, 1, la, GS1, st)),
                                  (3, lambda st: la_features(eng, st))])
            need(eng, la["gt"], NG1 - 1)
            eng.tensor_copy(G[:, :], PC[0:B * R, 0:D]).then_inc(s_midd, 1)
            need(eng, la["den"], NG1 - 1)
            eng.tensor_scalar(DENE[:, :], DEN[:, :], EPS_Z, None, ALU.add).then_inc(s_midd, 1)
            eng.wait_ge(s_midd, 2)
            eng.reciprocal(Z[:, :], DENE[:, :]).then_inc(s_midd, 1)
            eng.wait_ge(s_mid, 1)
            eng.tensor_copy(GT[:, :], bank(PC, 1, B * R)).then_inc(s_midd, 1)
            eng.wait_ge(s_mid, 2)
            eng.tensor_copy(KV[:, :], PC[0:B * R, 0:D]).then_inc(s_midd, 1)
            eng.wait_ge(s_midd, 5)
            run_groups(eng, NG1, [(0, lambda st: lb_x2(eng, st)), (3, lambda st: gate_add(eng, lb, GS1, st))])
            route_dve(eng, 1)
            ffn_dve(eng, 1)

        def busy(eng, n):
            for _ in range(n):
                eng.matmul(bank(PB, 1, P), ident[:, :], ident[:, :], start=True, stop=True)

        @block.tensor
        def _(eng):
            ahead(eng, l0, "xT mm")
            ahead(eng, la, "xT mm gt qt")
            ahead(eng, lb, "num xT mm")
            for f in range(2):
                ahead(eng, ffn[f], "xT up down")
            eng.wait_ge(s_const, 11)
            eng.wait_ge(s_constd, 11)
            eng.wait_ge(s_w["wg"], 16)
            eng.wait_ge(s_st, 3 * T0 // 4)
            busy(eng, 10)
            run_groups(eng, NG0, [(0, lambda st: ln_turn(eng, l0, GS0, PA_BANKS, st)),
                                  (1, lambda st: gate_mm(eng, l0, GS0, st))])
            for n in ("wq", "wk", "wv", "pr", "b1"):
                eng.wait_ge(s_w[n], 16)
            eng.matmul(PD[:, 0:R], Wk[:, :], Pr[:, :], start=True, stop=True)
            eng.matmul(PD[:, R:2 * R], Wq[:, :], Pr[:, :], start=True, stop=True)
            eng.transpose(PD[:, BANK:BANK + D], Wv[:, :], ident[:, :])
            eng.transpose(PD[:, 2 * R:2 * R + NE * NC], B1r[:, :], ident[0:NE * NC, 0:NE * NC]).then_inc(s_fold, 1)
            route_pe(eng, 0)
            eng.wait_ge(s_foldd, 4)
            ffn_pe(eng, 0)
            busy(eng, 16)
            need(eng, ffn[0]["out"], T1 - 1)
            eng.matmul(PC[0:B * R, 0:D], zeros[:, 0:B * R], zeros[:, 0:D], start=True, stop=False)
            run_groups(eng, NG1, [(1, lambda st: la_mm(eng, st)), (0, lambda st: ln_turn(eng, la, GS1, [PA], st)),
                                  (3, lambda st: la_sum(eng, st))])
            eng.wait_ge(s_midd, 1)
            eng.transpose(bank(PC, 1, B * R), G[:, :], ident[0:B * R, 0:B * R]).then_inc(s_mid, 1)
            eng.wait_ge(s_midd, 4)
            eng.matmul(PC[0:B * R, 0:D], GT[:, :], WvT[:, :], start=True, stop=True).then_inc(s_mid, 1)
            eng.wait_ge(s_midd, 5)
            need(eng, la["qts"], NG1 - 1)
            run_groups(eng, NG1, [(0, lambda st: lb_num(eng, st)), (2, lambda st: ln_turn(eng, lb, GS1, [PA], st)),
                                  (3, lambda st: gate_mm(eng, lb, GS1, st))])
            route_pe(eng, 1)
            eng.wait_ge(s_rd[1], AT[1]["done"])
            busy(eng, 10)
            ffn_pe(eng, 1)

        @block.scalar
        def _(eng):
            ahead(eng, l0, "xTs")
            ahead(eng, la, "xTs kx qts")
            ahead(eng, lb, "xn xTs")
            for f in range(2):
                ahead(eng, ffn[f], "xTs hT")
            w1_v, w2_v, b2_v = (a[:, :].rearrange("p (e f) -> p e f", e=NE) for a in (W1, W2, B2))
            eng.wait_ge(s_xload[0], 16)
            eng.dma_start(w1_v[:, :, 0:F], w1.rearrange("e d f -> d e f")).then_inc(s_w["w1"], 16)
            for e in range(NE):
                eng.dma_start(w2_v[:, e, 0:F].rearrange("p (c d) -> p c d", c=NC),
                              w2[e, :, :].rearrange("(c p) d -> p c d", p=P)).then_inc(s_w["w2"], 16)
            eng.dma_start(b2_v[:, :, 0:D], b2.unsqueeze(0).to_broadcast([P, NE, D])).then_inc(s_w["b2"], 16)

            def warm_up(function):
                eng.activation(warm[:, :], neghalf[:, 0:1], function).then_inc(s_warm, 1)
            eng.wait_ge(s_const, 4)
            warm_up(ACT.Copy)
            run_groups(eng, NG0, [(0, lambda st: ln_copy(eng, l0, GS0, PA_BANKS, st))])
            warm_up(ACT.Gelu)
            ffn_act(eng, 0)
            warm_up(ACT.Exp)
            run_groups(eng, NG1, [(1, lambda st: la_act_exp(eng, st)),
                                  (0, lambda st: ln_copy(eng, la, GS1, [PA], st)),
                                  (3, lambda st: la_act_q(eng, st))])
            run_groups(eng, NG1, [(0, lambda st: lb_norm(eng, st)),
                                  (1, lambda st: ln_copy(eng, lb, GS1, [PA], st))])
            warm_up(ACT.Gelu)
            ffn_act(eng, 1)


_INS = ['L0_attn_x', 'L0_attn_Wq', 'L0_attn_Wk', 'L0_attn_Wv', 'L0_attn_proj',
        'L0_ffn_W1', 'L0_ffn_b1', 'L0_ffn_W2', 'L0_ffn_b2', 'L0_ffn_Wg', 'L0_ffn_bg']


def kernel(**inputs):
    import numpy as _np
    import concourse.bacc as _bacc
    from concourse import mybir as _mybir
    from concourse.bass_utils import run_bass_kernel_spmd as _run

    nc = _bacc.Bacc("TRN2", target_bir_lowering=False, num_devices=1)
    arrays, args = {}, []
    for name in _INS:
        a = _np.ascontiguousarray(inputs[name])
        arrays[f"in_{name}_dram"] = a
        args.append(nc.dram_tensor(f"in_{name}_dram", a.shape, _mybir.dt.from_np(a.dtype), kind="ExternalInput").ap())
    shape = arrays["in_L0_attn_x_dram"].shape
    args.append(nc.dram_tensor("out_0_dram", shape, _mybir.dt.float32, kind="ExternalOutput").ap())
    build(nc, *args)
    r = _run(nc, [arrays], core_ids=[0])
    return r.results[0]["out_0_dram"]
```
